# Optimizing a Trainium2 kernel written in Bass

```python
import numpy as np
import jax
import jax.numpy as jnp

def _softmax(x, axis=-1):
    return jax.nn.softmax(x, axis=axis)

def _gelu(x):
    return jax.nn.gelu(x, approximate=True)

def _silu(x):
    return jax.nn.silu(x)

def _sigmoid(x):
    return jax.nn.sigmoid(x)

def _layernorm(x, axis=-1, eps=1e-05):
    m = jnp.mean(x, axis=axis, keepdims=True)
    v = jnp.var(x, axis=axis, keepdims=True)
    return (x - m) / jnp.sqrt(v + eps)

def _scatter_add(tgt, idx, src, axis=0):
    return tgt.at[idx].add(src)

def _segment_sum(src, seg, n):
    return jax.ops.segment_sum(src, seg, n)
kernel_name = 'mk_conv_preact_d2_conv_nchw64_r2_6a9a82'

def setup_inputs(seed: int=0):
    np.random.seed(seed)
    _w = jnp.asarray

    def _rec_inputs():
        import jax
        import jax.numpy as jnp
        _gk = jax.random.key(seed)
        x = 7.22e-05 + 1 * jax.random.normal(jax.random.fold_in(_gk, 1), (8, 32, 64, 64), jnp.float32)
        return x
    x = _rec_inputs()

    def _L0_conv_setup():
        import jax, jax.numpy as jnp
        import numpy as np
        from jax import lax
        DN = ('NCHW', 'OIHW', 'NCHW')
        key = jax.random.key(seed)
        ks = jax.random.split(key, 7)
        B, IC, OC, H, W = (8, 32, 32, 64, 64)
        return {'x': jax.random.normal(ks[0], (B, IC, H, W), jnp.float32), 'w3': jax.random.normal(ks[1], (OC, IC, 3, 3), jnp.float32) * 0.05, 'b3': jax.random.normal(ks[2], (OC,), jnp.float32) * 0.05, 'w5': jax.random.normal(ks[3], (OC, IC, 5, 5), jnp.float32) * 0.05, 'b5': jax.random.normal(ks[4], (OC,), jnp.float32) * 0.05, 'wr': jax.random.normal(ks[5], (OC, 10, 1, 1), jnp.float32) * 0.1, 'br': jax.random.normal(ks[6], (OC,), jnp.float32) * 0.05}
    _L0_conv_all = _L0_conv_setup()
    _L0_conv_in = {k: v for k, v in _L0_conv_all.items() if k in ('w3', 'b3', 'w5', 'b5', 'wr', 'br')}
    del _L0_conv_all

    def _L1_conv_setup():
        import jax, jax.numpy as jnp
        import numpy as np
        K = 3
        P = 1
        S = 1

        def _extract_patches(x, k, p, s):
            B, C, H, W = x.shape
            xp = jnp.pad(x, ((0, 0), (0, 0), (p, p), (p, p)))
            Ho = (H + 2 * p - k) // s + 1
            Wo = (W + 2 * p - k) // s + 1
            pats = [xp[:, :, dy:dy + Ho * s:s, dx:dx + Wo * s:s] for dy in range(k) for dx in range(k)]
            return jnp.stack(pats, axis=-1)
        key = jax.random.key(seed)
        k1, k2 = jax.random.split(key)
        x = jax.random.normal(k1, (16, 32, 32, 32), dtype=jnp.float32)
        filters = jax.random.normal(k2, (32, 32, 10, 10), dtype=jnp.float32) * 0.05
        return {'x': x, 'filters': filters}
    _L1_conv_all = _L1_conv_setup()
    _L1_conv_in = {k: v for k, v in _L1_conv_all.items() if k in ('filters',)}
    del _L1_conv_all
    return {'x': x, 'L0_conv_w3': _L0_conv_in['w3'], 'L0_conv_b3': _L0_conv_in['b3'], 'L0_conv_w5': _L0_conv_in['w5'], 'L0_conv_b5': _L0_conv_in['b5'], 'L0_conv_wr': _L0_conv_in['wr'], 'L0_conv_br': _L0_conv_in['br'], 'L1_conv_filters': _L1_conv_in['filters']}

def reference(x, L0_conv_w3, L0_conv_b3, L0_conv_w5, L0_conv_b5, L0_conv_wr, L0_conv_br, L1_conv_filters):
    import jax
    import jax.numpy as jnp

    def _L0_conv_ref(x, w3, b3, w5, b5, wr, br):
        import jax, jax.numpy as jnp
        import numpy as np
        from jax import lax
        DN = ('NCHW', 'OIHW', 'NCHW')
        y3 = lax.conv_general_dilated(x, w3, (1, 1), 'SAME', dimension_numbers=DN) + b3[None, :, None, None]
        y5 = lax.conv_general_dilated(x, w5, (1, 1), 'SAME', dimension_numbers=DN) + b5[None, :, None, None]
        B, C, H, W = y3.shape
        P = jnp.pad(y3, ((0, 0), (0, 0), (1, 1), (1, 1)))
        shifts = [P[:, :, 2 - sw:2 - sw + H, 2 - sh:2 - sh + W] for sh in range(3) for sw in range(3)]
        stacked = jnp.stack([y5] + shifts, axis=2)
        out = jnp.einsum('bcghw,cg->bchw', stacked, wr[:, :, 0, 0]) + br[None, :, None, None]
        return out

    def _L1_conv_ref(x, filters):
        import jax, jax.numpy as jnp
        import numpy as np
        K = 3
        P = 1
        S = 1

        def _extract_patches(x, k, p, s):
            B, C, H, W = x.shape
            xp = jnp.pad(x, ((0, 0), (0, 0), (p, p), (p, p)))
            Ho = (H + 2 * p - k) // s + 1
            Wo = (W + 2 * p - k) // s + 1
            pats = [xp[:, :, dy:dy + Ho * s:s, dx:dx + Wo * s:s] for dy in range(k) for dx in range(k)]
            return jnp.stack(pats, axis=-1)
        O, C, M, _ = filters.shape
        spot = _extract_patches(x, K, P, S)
        ones = jnp.ones(spot.shape[:-1] + (1,), dtype=spot.dtype)
        spot = jnp.concatenate([ones, spot], axis=-1)
        feat = (spot[..., :, None] * spot[..., None, :]).reshape(spot.shape[:-1] + (M * M,))
        out = jnp.einsum('bcyxf,ocf->boyx', feat, filters.reshape(O, C, M * M))
        return out

    def _gn(v, G=32, eps=1e-05):
        B_, C_, H_, W_ = v.shape
        g = v.reshape(B_, G, C_ // G, H_, W_)
        m = jnp.mean(g, axis=(2, 3, 4), keepdims=True)
        s = jnp.var(g, axis=(2, 3, 4), keepdims=True)
        return ((g - m) / jnp.sqrt(s + eps)).reshape(v.shape)

    def _ln_c(v, eps=1e-06):
        m = jnp.mean(v, axis=1, keepdims=True)
        s = jnp.var(v, axis=1, keepdims=True)
        return (v - m) / jnp.sqrt(s + eps)

    def _ln_t(v, eps=1e-05):
        m = jnp.mean(v, axis=-1, keepdims=True)
        s = jnp.var(v, axis=-1, keepdims=True)
        return (v - m) / jnp.sqrt(s + eps)

    def _to_tokens(v):
        B_, C_, H_, W_ = v.shape
        return v.reshape(B_, C_, H_ * W_).transpose(0, 2, 1)

    def _from_tokens(t, like):
        B_, C_, H_, W_ = like.shape
        return t.transpose(0, 2, 1).reshape(B_, C_, H_, W_)
    x = x + _L0_conv_ref(_gn(x), L0_conv_w3, L0_conv_b3, L0_conv_w5, L0_conv_b5, L0_conv_wr, L0_conv_br)
    x = x + _L1_conv_ref(_gn(x), L1_conv_filters)
    return x

_drawn_inputs = setup_inputs


def setup_inputs(seed=0):
    import zlib

    import numpy as np

    out = dict(_drawn_inputs(seed))
    spreads = {}
    factors = {'L0_conv_b3': 8.0, 'L0_conv_b5': 35.641, 'L0_conv_br': 2.978}
    for name, (base, spread) in spreads.items():
        noise = np.random.default_rng([zlib.crc32(name.encode()), seed]).standard_normal(out[name].shape)
        drawn = base * np.exp(spread * noise) if base else spread * noise
        out[name] = jnp.asarray(drawn.astype(out[name].dtype))
    for name, factor in factors.items():
        out[name] = (out[name] * factor).astype(out[name].dtype)
    return out
```

```python
from contextlib import ExitStack

import concourse.bass as bass
from concourse import mybir

B, C, H, W = 8, 32, 64, 64
SLOTS = 4
GROUP = 4
PITCH = W + 2
PIX = H * W
LAST = (H - 1) * PITCH + W - 1
QROWS = H // 4
CROWS = 8
NCH = QROWS // CROWS
GN_EPS = 1e-5


def flat(p):
    return p[0] * PITCH + p[1]


CONV0_SHIFTS = ((0, 0), (0, 1), (2, 0), (3, 0))
CONV0_READS = ((-2, -2), (-2, -1), (-2, 1), (-1, -2), (-1, 0), (-1, 2), (0, -1), (0, 1))


def conv0_taps():
    seen, out = set(), []
    for o in CONV0_READS:
        mine = []
        for a, s in enumerate(CONV0_SHIFTS):
            tap = (o[0] + s[0], o[1] + s[1])
            if max(abs(tap[0]), abs(tap[1])) <= 2 and tap not in seen:
                seen.add(tap)
                mine.append((a, tap))
        out.append((o, mine))
    assert len(seen) == 25
    return out


ROW_EDGE = (((0, -2), ((0, -2), (1, -1))), ((0, 0), ((0, 0), (1, 1))), ((0, 2), ((0, 2),)))
COL_EDGE = (((-2, 0), ((0, -2), (2, 0), (3, 1))), ((-1, 0), ((0, -1), (3, 2))))

SHIFTS = {
    "a": ((-1, -1), (-1, -2), (-1, -3), (-2, -2)),
    "b": ((-1, 0), (1, -2), (-1, 0), (0, -2)),
    "c": ((-2, -3), (-2, -2), (-2, -2), (-2, -2)),
}
PRODUCTS = (
    ("b", "c", (1, 2), ((0, 1), (1, 1), (1, -1))),
    ("a", "c", (1, 0), ((2, 2), (2, 3), (0, 2), (1, 2), (2, 1), (0, 1))),
    ("a", "c", (2, 1), ((1, 2), (1, 1), (0, 2), (0, 1))),
    ("a", "c", (-1, 0), ((2, 2), (2, 3), (2, 1))),
)
LINEAR_READS = ((1, 2), (2, 2), (0, 2))


def inside(p):
    return abs(p[0]) <= 1 and abs(p[1]) <= 1


def conv1_taps():
    seen, out = set(), []
    for u, v, d, reads in PRODUCTS:
        rows = []
        for o in reads:
            mine = []
            for a in range(SLOTS):
                i = (o[0] + SHIFTS[u][a][0], o[1] + SHIFTS[u][a][1])
                j = (o[0] + SHIFTS[v][a][0] + d[0], o[1] + SHIFTS[v][a][1] + d[1])
                pair = tuple(sorted((i, j)))
                if inside(i) and inside(j) and pair not in seen:
                    seen.add(pair)
                    mine.append((a, i, j))
            rows.append(mine)
        out.append(rows)
    assert len(seen) == 45
    lin, linear = set(), []
    for o in LINEAR_READS:
        mine = []
        for a in range(SLOTS):
            i = (o[0] + SHIFTS["a"][a][0], o[1] + SHIFTS["a"][a][1])
            if inside(i) and i not in lin:
                lin.add(i)
                mine.append((a, i))
        linear.append(mine)
    assert len(lin) == 9
    return out, linear


def ranges():
    need = {"g": [(min(map(flat, CONV0_READS)), LAST + max(map(flat, CONV0_READS)))],
            "a": [(min(map(flat, LINEAR_READS)), LAST + max(map(flat, LINEAR_READS)))], "b": [], "c": []}
    need["g"].append((-2 * PITCH, LAST + 2))
    products = []
    for u, v, d, reads in PRODUCTS:
        lo, hi = min(map(flat, reads)), LAST + max(map(flat, reads))
        products.append((lo, hi))
        need[u].append((lo, hi))
        need[v].append((lo + flat(d), hi + flat(d)))
    span = {k: (min(lo for lo, _ in r), max(hi for _, hi in r)) for k, r in need.items()}
    shifts = dict(SHIFTS, g=CONV0_SHIFTS)
    plane = (min(span[k][0] + flat(s) for k in span for s in shifts[k]),
             max(span[k][1] + flat(s) for k in span for s in shifts[k]))
    return span, products, plane


def conv_kernel(nc, x, w3, b3, w5, b5, wr, br, filters, out):
    fp32 = mybir.dt.float32
    ALU = mybir.AluOpType
    ACT = mybir.ActivationFunctionType

    span, product_span, (plane_lo, plane_hi) = ranges()
    plane_len = plane_hi - plane_lo + 1
    size = {k: hi - lo + 1 for k, (lo, hi) in span.items()}
    taps0 = conv0_taps()
    taps1, linear1 = conv1_taps()
    n_product_reads = sum(len(p[3]) for p in PRODUCTS)
    M = filters.shape[2]
    N_READS = n_product_reads + len(LINEAR_READS)
    SLOT_DMA = 16 * SLOTS
    AHEAD = 2
    N_PRODUCTS = len(PRODUCTS)

    ctx = ExitStack()
    with ctx:
        def sb(name, shape):
            return ctx.enter_context(nc.sbuf_tensor(name, shape, fp32))

        def sem(name):
            return ctx.enter_context(nc.semaphore(name))

        raw = sb("raw", [128, PIX])
        plane = sb("plane", [128, plane_len])
        stack_a = [sb(f"stack_a{i}", [128, max(size["a"], size["g"]) + PITCH - W]) for i in range(2)]
        stack_b = sb("stack_b", [128, size["b"]])
        stack_c = [sb(f"stack_c{i}", [128, size["c"]]) for i in range(2)]
        product = [sb(f"product{i}", [128, max(hi - lo + 1 for lo, hi in product_span) + PITCH - W]) for i in range(2)]
        resid = sb("resid", [128, B, QROWS * W])
        bias_map = sb("bias_map", [128, QROWS, W])
        weight0 = sb("weight0", [128, len(taps0), C])
        n_edges = 2 * len(ROW_EDGE) + 2 * len(COL_EDGE) + 4
        weight_edge = sb("weight_edge", [128, n_edges, C])
        weight1 = sb("weight1", [128, n_product_reads + len(LINEAR_READS) + 1, C])
        ones = sb("ones", [128, 2])
        const1 = sb("const1", [128, 2])
        wr_rows = sb("wr_rows", [C, C * 10])
        wr_out = sb("wr_out", [128, 10])
        b_out = sb("b_out", [128, 3])
        ring_bias = sb("ring_bias", [128, 16])
        stats = sb("stats", [128, PIX // 512, 6])
        mean_var = sb("mean_var", [128, 2])
        norm = sb("norm", [128, 8])
        filt = product[0][0:C, 0:C * M * M].rearrange("p (o m) -> p o m", o=C)
        scratch = product[1]
        w3_in = scratch[0:C, 0:288].rearrange("p (o t) -> p o t", o=C)
        w5_in = scratch[0:C, 288:288 + 800].rearrange("p (o t) -> p o t", o=C)
        w5_sum = stack_c[1][0:C, 0:800].rearrange("p (o y x) -> p o y x", o=C, y=5)
        shift_w3 = [stack_c[0][0:C, 288 * e:288 * e + 288].rearrange("p (o y x) -> p o y x", o=C, y=3)
                    for e in range(9)]
        edge_w = [stack_c[1][0:C, 800 + 160 * e:960 + 160 * e].rearrange("p (o t) -> p o t", o=C)
                  for e in range(4)]

        acc0 = ctx.enter_context(nc.psum_tensor("acc0", [128, 2, NCH * CROWS * W], fp32))
        acc1 = ctx.enter_context(nc.psum_tensor("acc1", [128, 2, NCH * CROWS * W], fp32))

        weights_in = sem("weights_in")
        filters_in = sem("filters_in")
        bias_in = sem("bias_in")
        raw_in = sem("raw_in")
        x1_in = sem("x1_in")
        resid_in = sem("resid_in")
        plane_zero = sem("plane_zero")
        weights_zero = sem("weights_zero")
        chain = sem("chain")
        var_ready = sem("var_ready")
        std_ready = sem("std_ready")
        plane_ready = sem("plane_ready")
        a_filled = [sem(f"a_filled{i}") for i in range(2)]
        b_filled = sem("b_filled")
        c_filled = [sem(f"c_filled{i}") for i in range(2)]
        weight0_ready = sem("weight0_ready")
        weight1_ready = sem("weight1_ready")
        const1_sum = sem("const1_sum")
        conv_done = sem("conv_done")
        x1_ready = sem("x1_ready")
        product_ready = sem("product_ready")
        product_used = sem("product_used")
        out_ready = sem("out_ready")
        stored = sem("stored")

        block = ctx.enter_context(nc.Block())

        def fill(eng, to, kind, bi, done):
            shifts = CONV0_SHIFTS if kind == "g" else SHIFTS[kind]
            lo, _ = span[kind]
            for a, s in enumerate(shifts):
                at = lo + flat(s) - plane_lo
                eng.dma_start(to[32 * a:32 * a + 32, 0:size[kind]],
                              plane[32 * bi:32 * bi + 32, at:at + size[kind]]).then_inc(done, 16)

        @block.sync
        def _(sp):
            sp.dma_start(raw[:, :], x[0:GROUP].rearrange("b c h w -> (b c) (h w)")).then_inc(raw_in, 16)
            with sp.Fori(0, B // GROUP) as g:
                sp.wait_ge(plane_ready, g + 1)
                for bi in range(GROUP):
                    sp.wait_ge(conv_done, g * GROUP + (bi + 1))
                    fill(sp, stack_a[bi % 2], "g", bi, a_filled[bi % 2])
            with sp.Fori(0, B // GROUP) as g:
                sp.wait_ge(plane_ready, g + (B // GROUP + 1))
                for bi in range(GROUP):
                    s = bi % 2
                    sp.wait_ge(product_ready, g * (GROUP * N_PRODUCTS) + ((AHEAD + bi - 1) * N_PRODUCTS + 1))
                    fill(sp, stack_b, "b", bi, b_filled)
                    sp.wait_ge(product_ready, g * (GROUP * N_PRODUCTS) + (AHEAD + bi - 1) * N_PRODUCTS)
                    fill(sp, stack_c[s], "c", bi, c_filled[s])
                    sp.wait_ge(conv_done, g * GROUP + (B + bi + 1))
                    fill(sp, stack_a[s], "a", bi, a_filled[s])

        @block.gpsimd
        def _(pool):
            nc.gpsimd.memset(plane[:, :], 0.0).then_inc(plane_zero, 1)
            nc.gpsimd.memset(ones[:, :], 1.0).then_inc(plane_zero, 1)
            for b in range(B):
                pool.wait_ge(out_ready, AHEAD + b + 1)
                for q in range(4):
                    pool.dma_start(out[b].rearrange("c (q r) w -> q c (r w)", q=4)[q],
                                   resid[32 * q:32 * q + 32, b, :]).then_inc(stored, 16)
            pool.wait_ge(stored, 16 * 4 * B)

        @block.scalar
        def _(act):
            act.dma_start(w3_in, w3.rearrange("o c y x -> c o (y x)")).then_inc(weights_in, 16)
            act.dma_start(wr_rows[:, :], wr.rearrange("o g y x -> (y x) (o g)").to_broadcast((C, C * 10)))\
               .then_inc(weights_in, 16)
            act.dma_start(w5_in, w5.rearrange("o c y x -> c o (y x)")).then_inc(weights_in, 16)
            for q in range(4):
                act.dma_start(wr_out[32 * q:32 * q + 32, :], wr.rearrange("o g y x -> o (g y x)"))\
                   .then_inc(bias_in, 16)
                for n, v in enumerate((b3, b5, br)):
                    act.dma_start(b_out[32 * q:32 * q + 32, n:n + 1], v.rearrange("(o n) -> o n", n=1))\
                       .then_inc(bias_in, 16)
            for q in range(4):
                act.dma_start(resid[32 * q:32 * q + 32, :, :],
                              x.rearrange("b c (q r) w -> q c b (r w)", q=4)[q]).then_inc(resid_in, 16)
            act.dma_start(filt, filters.rearrange("o c i j -> c o (i j)")).then_inc(filters_in, 16)

            def std(phase):
                act.wait_ge(var_ready, phase + 1)
                nc.scalar.activation(norm[:, 1:2], norm[:, 0:1], ACT.Sqrt).then_inc(std_ready, 1)

            std(0)
            act.wait_ge(plane_ready, 1)
            act.dma_start(raw[:, :], x[GROUP:B].rearrange("b c h w -> (b c) (h w)")).then_inc(raw_in, 16)
            std(1)
            for g in range(B // GROUP):
                act.wait_ge(plane_ready, g + 2)
                for bi in range(GROUP):
                    b = GROUP * g + bi
                    act.wait_ge(x1_ready, AHEAD + b + 1)
                    for q in range(4):
                        act.dma_start(raw[32 * bi:32 * bi + 32, q * QROWS * W:(q + 1) * QROWS * W],
                                      resid[32 * q:32 * q + 32, b, :]).then_inc(x1_in, 16)
                std(g + 2)

        @block.vector
        def _(dve):
            steps = [0]

            def step(ins):
                steps[0] += 1
                ins.then_inc(chain, 1)
                dve.wait_ge(chain, steps[0])

            def statistics():
                for n in range(PIX // 512):
                    ins = nc.vector.bn_stats(stats[:, n, :], raw[:, 512 * n:512 * n + 512])
                step(ins)
                step(nc.vector.bn_aggr(mean_var[:, :], stats[:, :, :].rearrange("p n s -> p (n s)")))
                nc.vector.tensor_scalar(norm[:, 0:1], mean_var[:, 1:2], GN_EPS, None, ALU.add)\
                    .then_inc(var_ready, 1)

            def normalise(phase):
                dve.wait_ge(std_ready, phase + 1)
                step(nc.vector.reciprocal(norm[:, 2:3], norm[:, 1:2]))
                step(nc.vector.scalar_tensor_tensor(norm[:, 3:4], norm[:, 2:3], norm[:, 2:3], norm[:, 0:1],
                                                    ALU.mult, ALU.mult))
                step(nc.vector.tensor_scalar(norm[:, 4:5], norm[:, 3:4], -0.5, 1.5, ALU.mult, ALU.add))
                step(nc.vector.tensor_tensor(norm[:, 5:6], norm[:, 2:3], norm[:, 4:5], ALU.mult))
                inner = plane[:, -plane_lo:-plane_lo + H * PITCH].rearrange("p (y x) -> p y x", x=PITCH)[:, :, 0:W]
                nc.vector.tensor_scalar(inner, raw[:, :].rearrange("p (y x) -> p y x", x=W),
                                        mean_var[:, 0:1], norm[:, 5:6], ALU.subtract, ALU.mult)\
                    .then_inc(plane_ready, 1)

            dve.sem_inc(x1_ready, AHEAD)
            dve.sem_inc(product_ready, AHEAD * N_PRODUCTS)
            nc.vector.memset(weight0[:, :, :], 0.0)
            step(nc.vector.memset(weight_edge[:, :, :], 0.0))
            step(nc.vector.memset(weight1[:, :, :], 0.0))
            for e in range(4):
                last = nc.vector.memset(edge_w[e], 0.0)
            step(last)
            dve.wait_ge(raw_in, 16)
            statistics()
            dve.wait_ge(plane_zero, 1)
            normalise(0)

            def r_rows(g, shape):
                v = wr_rows[:, :].rearrange("p (o g) -> p o g", g=10)[:, :, g:g + 1]
                return v.to_broadcast(shape)

            def shift_index(ey, ex):
                return 1 + 3 * (1 - ex) + (1 - ey)

            EY_EX = [(ey, ex) for ey in (-1, 0, 1) for ex in (-1, 0, 1)]
            dve.wait_ge(weights_in, 48)
            for e, (ey, ex) in enumerate(EY_EX):
                nc.vector.tensor_tensor(shift_w3[e].rearrange("p o y x -> p o (y x)"), w3_in,
                                        r_rows(shift_index(ey, ex), (C, C, 9)), ALU.mult)
            step(nc.vector.tensor_tensor(w5_sum.rearrange("p o y x -> p o (y x)"), w5_in,
                                         r_rows(0, (C, C, 25)), ALU.mult))
            for e, (ey, ex) in enumerate(EY_EX):
                window = w5_sum[:, :, ey + 1:ey + 4, ex + 1:ex + 4]
                step(nc.vector.tensor_tensor(window, window, shift_w3[e], ALU.add))
            for n, (_, mine) in enumerate(taps0):
                for a, (dy, dx) in mine:
                    last = nc.vector.tensor_copy(weight0[32 * a:32 * a + 32, n, :], w5_sum[:, :, dy + 2, dx + 2])
            last.then_inc(weight0_ready, 1)

            def shifted(ey, ex):
                return shift_w3[EY_EX.index((ey, ex))]

            for e in (-1, 0, 1):
                for side, add in ((0, shifted(-1, e)[:, :, 2, :]), (1, shifted(1, e)[:, :, 0, :]),
                                  (2, shifted(e, -1)[:, :, :, 2]), (3, shifted(e, 1)[:, :, :, 0])):
                    part = edge_w[side][:, :, e + 1:e + 4]
                    last = nc.vector.tensor_tensor(part, part, add, ALU.add)
                step(last)
            n = 0
            for side in range(4):
                for _, mine in (ROW_EDGE if side < 2 else COL_EDGE):
                    for a, t in mine:
                        nc.vector.tensor_scalar(weight_edge[32 * a:32 * a + 32, n, :],
                                                edge_w[side][:, :, t + 2], -1.0, None, ALU.mult)
                    n += 1
            for ey, ex in ((-1, -1), (-1, 1), (1, -1), (1, 1)):
                last = nc.vector.tensor_copy(weight_edge[0:32, n, :], shifted(ey, ex)[:, :, 1 - ey, 1 - ex])
                n += 1
            last.then_inc(weight0_ready, 1)

            dve.wait_ge(bias_in, 16 * 16)
            rb = ring_bias
            step(nc.vector.tensor_scalar(rb[:, 0:9], wr_out[:, 1:10], b_out[:, 0:1], None, ALU.mult))

            def ring(ey, ex):
                i = shift_index(ey, ex) - 1
                return rb[:, i:i + 1]

            step(nc.vector.reduce_sum(rb[:, 9:10], rb[:, 0:9], mybir.AxisListType.X))
            step(nc.vector.scalar_tensor_tensor(rb[:, 9:10], wr_out[:, 0:1], b_out[:, 1:2], rb[:, 9:10],
                                                ALU.mult, ALU.add))
            step(nc.vector.tensor_tensor(rb[:, 9:10], rb[:, 9:10], b_out[:, 2:3], ALU.add))
            for k, three in enumerate((((-1, -1), (-1, 0), (-1, 1)), ((1, -1), (1, 0), (1, 1)),
                                       ((-1, -1), (0, -1), (1, -1)), ((-1, 1), (0, 1), (1, 1)))):
                to = rb[:, 10 + k:11 + k]
                step(nc.vector.tensor_tensor(to, ring(*three[0]), ring(*three[1]), ALU.add))
                step(nc.vector.tensor_tensor(to, to, ring(*three[2]), ALU.add))
            step(nc.vector.memset(bias_map[:, :, :], 0.0))
            step(nc.vector.tensor_scalar(bias_map[:, :, :], bias_map[:, :, :], rb[:, 9:10], None, ALU.add))
            low, high = slice(0, 32), slice(96, 128)
            for p, region, k in ((slice(0, 128), (slice(None), slice(0, 1)), 12),
                                 (slice(0, 128), (slice(None), slice(W - 1, W)), 13),
                                 (low, (slice(0, 1), slice(None)), 10),
                                 (high, (slice(QROWS - 1, QROWS), slice(None)), 11)):
                part = bias_map[p, region[0], region[1]]
                step(nc.vector.tensor_scalar(part, part, rb[p, k:k + 1], None, ALU.subtract))
            for p, row, col, at in ((low, 0, 0, (-1, -1)), (low, 0, W - 1, (-1, 1)),
                                    (high, QROWS - 1, 0, (1, -1)), (high, QROWS - 1, W - 1, (1, 1))):
                part = bias_map[p, row, col:col + 1]
                i = shift_index(*at) - 1
                step(nc.vector.tensor_tensor(part, part, rb[p, i:i + 1], ALU.add))

            flat_bias = bias_map[:, :, :].rearrange("p y x -> p (y x)")
            dve.wait_ge(resid_in, 64)

            def finish0(b):
                step(nc.vector.tensor_tensor(resid[:, b, :], resid[:, b, :], flat_bias, ALU.add))
                dve.wait_ge(conv_done, AHEAD + b + 1)
                nc.vector.tensor_tensor(resid[:, b, :], acc0[:, b % 2, :], resid[:, b, :], ALU.add)\
                    .then_inc(x1_ready, 1)

            def conv1_weights():
                def entry(i, j):
                    return filt[:, :, i * M + j]

                def tap(i):
                    return 1 + 3 * (i[0] + 1) + (i[1] + 1)

                dve.wait_ge(filters_in, 16)
                n = 0
                for rows in taps1:
                    for mine in rows:
                        for a, i, j in mine:
                            to = weight1[32 * a:32 * a + 32, n, :]
                            if i == j:
                                nc.vector.tensor_copy(to, entry(tap(i), tap(i)))
                            else:
                                nc.vector.tensor_tensor(to, entry(tap(i), tap(j)), entry(tap(j), tap(i)), ALU.add)
                        n += 1
                for mine in linear1:
                    for a, i in mine:
                        nc.vector.tensor_tensor(weight1[32 * a:32 * a + 32, n, :],
                                                entry(0, tap(i)), entry(tap(i), 0), ALU.add)
                    n += 1
                nc.vector.tensor_copy(weight1[0:32, n, :], entry(0, 0)).then_inc(weight1_ready, 1)

            def planes_copied(a_fills, bc_fills):
                for s in range(2):
                    dve.wait_ge(a_filled[s], SLOT_DMA * a_fills)
                    if bc_fills:
                        dve.wait_ge(c_filled[s], SLOT_DMA * bc_fills)
                if bc_fills:
                    dve.wait_ge(b_filled, SLOT_DMA * 2 * bc_fills)

            dve.wait_ge(raw_in, 32)
            statistics()
            finish0(0)
            conv1_weights()
            finish0(1)
            planes_copied(2, 0)
            normalise(1)
            for b in range(2, 6):
                finish0(b)
            dve.wait_ge(x1_in, 16 * 16)
            statistics()
            planes_copied(4, 0)
            normalise(2)
            finish0(6)
            finish0(7)
            dve.wait_ge(const1_sum, 1)
            nc.vector.tensor_copy(const1[:, :], acc1[:, 1, 0:2]).then_inc(out_ready, AHEAD)

            def multiply(b, k):
                u, v, d, reads = PRODUCTS[k]
                lo, hi = product_span[k]
                n = len(PRODUCTS) * b + k
                at = {"a": stack_a[b % 2], "b": stack_b, "c": stack_c[b % 2]}
                if n >= 2:
                    dve.wait_ge(product_used, n - 1)
                first = at[u][:, lo - span[u][0]:hi + 1 - span[u][0]]
                second = at[v][:, lo + flat(d) - span[v][0]:hi + 1 + flat(d) - span[v][0]]
                return nc.vector.tensor_tensor(product[n % 2][:, 0:hi - lo + 1], first, second, ALU.mult)

            def finish1(b):
                dve.wait_ge(conv_done, AHEAD + B + b + 1)
                nc.vector.scalar_tensor_tensor(resid[:, b, :], acc1[:, b % 2, :], const1[:, 0:1], resid[:, b, :],
                                               ALU.add, ALU.add).then_inc(out_ready, 1)

            for b in range(B):
                s = b % 2
                if b == GROUP:
                    dve.wait_ge(x1_in, 32 * 16)
                    statistics()
                    planes_copied(6, 2)
                    normalise(3)
                dve.wait_ge(b_filled, SLOT_DMA * (b + 1))
                dve.wait_ge(c_filled[s], SLOT_DMA * (b // 2 + 1))
                multiply(b, 0).then_inc(product_ready, 1)
                dve.wait_ge(a_filled[s], SLOT_DMA * (B // 2 + b // 2 + 1))
                multiply(b, 1).then_inc(product_ready, 1)
                if b >= 1:
                    finish1(b - 1)
                multiply(b, 2).then_inc(product_ready, 1)
                multiply(b, 3).then_inc(product_ready, 1)
            finish1(B - 1)

        @block.tensor
        def _(pe):
            def pixels(stack, base, q, h):
                at = base + (QROWS * q + CROWS * h) * PITCH
                return stack[:, at:at + CROWS * PITCH].rearrange("p (y x) -> p y x", x=PITCH)[:, :, 0:W]

            def acc_rows(acc, s, q, h):
                return acc[32 * q:32 * q + 32, s, 512 * h:512 * h + 512]

            def tap_all(acc, s, weights, stack, base, start, stop):
                for h in range(NCH):
                    for q in range(4):
                        last = nc.tensor.matmul(acc_rows(acc, s, q, h), weights, pixels(stack, base, q, h),
                                                start=start, stop=stop, tile_position=(0, 32 * q))
                return last

            g_lo = span["g"][0]

            def edges(s, stack):
                n = 0
                for side in range(2):
                    q, h, row = (0, 0, 0) if side == 0 else (3, NCH - 1, CROWS - 1)
                    y = 0 if side == 0 else H - 1
                    for o, _ in ROW_EDGE:
                        at = flat((y, 0)) + flat(o) - g_lo
                        width = W - max(0, o[1]) if side == 1 else W
                        nc.tensor.matmul(acc0[32 * q:32 * q + 32, s, 512 * h + row * W:512 * h + row * W + width],
                                         weight_edge[:, n, :], stack[:, at:at + width],
                                         start=False, stop=False, tile_position=(0, 32 * q))
                        n += 1
                for side in range(2):
                    col = 0 if side == 0 else W - 1
                    for o, _ in COL_EDGE:
                        for h in range(NCH):
                            for q in range(4):
                                at = flat((QROWS * q + CROWS * h, col)) + flat(o) - g_lo
                                nc.tensor.matmul(acc_rows(acc0, s, q, h)[:, col:col + (CROWS - 1) * W + 1:W],
                                                 weight_edge[:, n, :],
                                                 stack[:, at:at + (CROWS - 1) * PITCH + 1:PITCH],
                                                 start=False, stop=False, tile_position=(0, 32 * q))
                        n += 1
                for q, h, row, y in ((0, 0, 0, 0), (3, NCH - 1, CROWS - 1, H - 1)):
                    for col in (0, W - 1):
                        at = flat((y, col)) - g_lo
                        nc.tensor.matmul(acc0[32 * q:32 * q + 32, s, 512 * h + row * W + col:512 * h + row * W + col + 1],
                                         weight_edge[:, n, :], stack[:, at:at + 1],
                                         start=False, stop=False, tile_position=(0, 32 * q))
                        n += 1

            pe.sem_inc(conv_done, AHEAD)
            pe.wait_ge(weight0_ready, 1)
            with pe.Fori(0, B // 2) as i:
                for s in range(2):
                    pe.wait_ge(a_filled[s], i * SLOT_DMA + SLOT_DMA)
                    pe.wait_ge(x1_ready, i * 2 + (s + 1))
                    for n, (o, _) in enumerate(taps0):
                        if n == len(taps0) - 1:
                            pe.wait_ge(weight0_ready, 2)
                            edges(s, stack_a[s])
                        last = tap_all(acc0, s, weight0[:, n, :], stack_a[s], flat(o) - g_lo,
                                       n == 0, n == len(taps0) - 1)
                    last.then_inc(conv_done, 1)

            pe.wait_ge(weight1_ready, 1)
            pe.wait_ge(plane_zero, 2)
            for q in range(4):
                last = nc.tensor.matmul(acc1[32 * q:32 * q + 32, 1, 0:2], weight1[:, N_READS, :], ones[:, :],
                                        start=True, stop=True, tile_position=(0, 32 * q))
            last.then_inc(const1_sum, 1)

            with pe.Fori(0, B // 2) as i:
                for s in range(2):
                    n = 0
                    pe.wait_ge(out_ready, i * 2 + (s + 1))
                    for k, (_, _, _, reads) in enumerate(PRODUCTS):
                        pe.wait_ge(product_ready, i * (2 * N_PRODUCTS) + ((AHEAD + s) * N_PRODUCTS + k + 1))
                        for o in reads:
                            last = tap_all(acc1, s, weight1[:, n, :], product[k % 2], flat(o) - product_span[k][0],
                                           n == 0, False)
                            n += 1
                        last.then_inc(product_used, 1)
                    for o in LINEAR_READS:
                        last = tap_all(acc1, s, weight1[:, n, :], stack_a[s], flat(o) - span["a"][0],
                                       False, o == LINEAR_READS[-1])
                        n += 1
                    last.then_inc(conv_done, 1)


def kernel(**inputs):
    import numpy as np
    import concourse.bacc as bacc
    from concourse.bass_utils import run_bass_kernel_spmd

    nc = bacc.Bacc("TRN2", target_bir_lowering=False, num_devices=1)
    names = ("x", "L0_conv_w3", "L0_conv_b3", "L0_conv_w5", "L0_conv_b5", "L0_conv_wr", "L0_conv_br",
             "L1_conv_filters")
    arrays, args = {}, []
    for name in names:
        a = np.ascontiguousarray(inputs[name])
        arrays[f"in_{name}"] = a
        args.append(nc.dram_tensor(f"in_{name}", a.shape, mybir.dt.from_np(a.dtype), kind="ExternalInput").ap())
    out = nc.dram_tensor("out", (B, C, H, W), mybir.dt.float32, kind="ExternalOutput").ap()
    conv_kernel(nc, *args, out)
    r = run_bass_kernel_spmd(nc, [arrays], core_ids=[0])
    return r.results[0]["out"]
```

```python
from contextlib import ExitStack

import concourse.bass as bass
from concourse import mybir

B, C, H, W = 8, 32, 64, 64
SLOTS = 4
GROUP = 4
PITCH = W + 2
PIX = H * W
LAST = (H - 1) * PITCH + W - 1
QROWS = H // 4
CROWS = 8
NCH = QROWS // CROWS
GN_EPS = 1e-5


def flat(p):
    return p[0] * PITCH + p[1]


CONV0_SHIFTS = {"g": ((0, 0), (0, 1), (1, 1), (1, 2)), "h": ((-2, 0), (0, 0), (2, 0))}
CONV0_READS = (("g", (-2, -1)), ("g", (-2, 1)), ("h", (0, -2)), ("g", (-1, -2)), ("g", (0, 1)), ("g", (1, -2)),
               ("g", (1, 0)))


def conv0_taps():
    seen, out = set(), []
    for kind, o in CONV0_READS:
        mine = []
        for a, s in enumerate(CONV0_SHIFTS[kind]):
            tap = (o[0] + s[0], o[1] + s[1])
            if max(abs(tap[0]), abs(tap[1])) <= 2 and tap not in seen:
                seen.add(tap)
                mine.append((a, tap))
        out.append((kind, o, mine))
    assert len(seen) == 25
    return out


ROW_EDGE = (((0, -2), ((0, -2), (1, -1))), ((0, 0), ((0, 0), (1, 1))), ((0, 2), ((0, 2),)))
COL_EDGE = (((0, 0), ((0, -2), (1, 0), (2, 2))), ((1, 0), ((0, -1), (1, 1))))

SHIFTS = {
    "a": ((-1, 0), (-1, -1), (-1, -1), (-1, 1)),
    "c": ((0, 1), (0, 1), (0, 2), (0, 1)),
    "b": ((-1, -1), (-1, 1)),
}
PRODUCTS = (
    ((((0, 4), "a", "c", (0, -2)),), ((1, 0), (0, 0), (1, 1), (0, 1))),
    ((((0, 4), "a", "c", (-3, -2)),), ((2, 0), (2, 1))),
    ((((0, 2), "b", "c", (0, 0)), ((2, 4), "a", "a", (0, 0))), ((0, 0), (1, 0), (2, 0))),
    ((((0, 4), "a", "c", (-1, -1)),), ((0, 0), (1, 0), (2, 0))),
    ((((0, 4), "c", "a", (3, 0)),), ((-1, 0),)),
)
SQUARED = 2
LINEAR_READS = ((0, 0), (1, 0), (2, 0))
LINEAR_AFTER = (0, 1, 0, 0, 2)

ON_SCALAR = {"g": (2, 3), "h": (2,), "a": (3,), "c": (3,), "b": (1,)}


def inside(p):
    return abs(p[0]) <= 1 and abs(p[1]) <= 1


def conv1_taps():
    seen, out = set(), []
    for parts, reads in PRODUCTS:
        rows = []
        for o in reads:
            mine = []
            for (first, end), u, v, d in parts:
                for a in range(first, end):
                    i = (o[0] + SHIFTS[u][a][0], o[1] + SHIFTS[u][a][1])
                    j = (o[0] + SHIFTS[v][a][0] + d[0], o[1] + SHIFTS[v][a][1] + d[1])
                    pair = tuple(sorted((i, j)))
                    if inside(i) and inside(j) and pair not in seen:
                        seen.add(pair)
                        mine.append((a, i, j))
            rows.append(mine)
        out.append(rows)
    assert len(seen) == 45
    lin, linear = set(), []
    for o in LINEAR_READS:
        mine = []
        for a in range(SLOTS):
            i = (o[0] + SHIFTS["a"][a][0], o[1] + SHIFTS["a"][a][1])
            if inside(i) and i not in lin:
                lin.add(i)
                mine.append((a, i))
        linear.append(mine)
    assert len(lin) == 9
    return out, linear


def ranges():
    need = {"g": [(-2, LAST + 2)], "h": [(0, LAST + flat((1, 0)))],
            "a": [(min(map(flat, LINEAR_READS)), LAST + max(map(flat, LINEAR_READS)))], "b": [], "c": []}
    for kind, o in CONV0_READS:
        need[kind].append((flat(o), LAST + flat(o)))
    products = []
    for parts, reads in PRODUCTS:
        lo, hi = min(map(flat, reads)), LAST + max(map(flat, reads))
        products.append((lo, hi))
        for _, u, v, d in parts:
            need[u].append((lo, hi))
            need[v].append((lo + flat(d), hi + flat(d)))
    span = {k: (min(lo for lo, _ in r), max(hi for _, hi in r)) for k, r in need.items()}
    shifts = dict(SHIFTS, **CONV0_SHIFTS)
    plane = (min(span[k][0] + flat(s) for k in span for s in shifts[k]),
             max(span[k][1] + flat(s) for k in span for s in shifts[k]))
    return span, products, plane


def conv_kernel(nc, x, w3, b3, w5, b5, wr, br, filters, out):
    fp32 = mybir.dt.float32
    ALU = mybir.AluOpType
    ACT = mybir.ActivationFunctionType

    span, product_span, (plane_lo, plane_hi) = ranges()
    plane_len = plane_hi - plane_lo + 1
    size = {k: hi - lo + 1 for k, (lo, hi) in span.items()}
    taps0 = conv0_taps()
    taps1, linear1 = conv1_taps()
    n_product_reads = sum(len(reads) for _, reads in PRODUCTS)
    M = filters.shape[2]
    N_READS = n_product_reads + len(LINEAR_READS)
    SLOT_DMA = 16 * SLOTS
    B_DMA = 16 * len(SHIFTS["b"])
    H_DMA = 16 * len(CONV0_SHIFTS["h"])
    AHEAD = 2
    CONV_AHEAD = 4
    RESID_PARTS = ((0, 2), (2, GROUP), (GROUP, B))
    PIECES = 4
    PIECE = PIX // PIECES
    N_PRODUCTS = len(PRODUCTS)

    ctx = ExitStack()
    with ctx:
        def sb(name, shape):
            return ctx.enter_context(nc.sbuf_tensor(name, shape, fp32))

        def sem(name):
            return ctx.enter_context(nc.semaphore(name))

        raw = sb("raw", [128, PIX])
        plane = sb("plane", [128, plane_len])
        stack_a = [sb(f"stack_a{i}", [128, max(size["a"], size["g"]) + PITCH - W]) for i in range(2)]
        stack_b = sb("stack_b", [128, max(size["b"], size["h"]) + PITCH - W])
        stack_c = [sb(f"stack_c{i}", [128, max(size["c"], size["g"]) + PITCH - W]) for i in range(2)]
        product = [sb(f"product{i}", [128, max(hi - lo + 1 for lo, hi in product_span) + PITCH - W]) for i in range(2)]
        stack_g = (stack_c[0], stack_a[0], stack_c[1], stack_a[1])
        stack_h = (stack_b, product[1])
        resid = sb("resid", [128, B, QROWS * W])
        bias_map = sb("bias_map", [128, QROWS, W])
        weight0 = sb("weight0", [128, len(taps0), C])
        n_edges = 2 * len(ROW_EDGE) + 2 * len(COL_EDGE) + 4
        weight_edge = sb("weight_edge", [128, n_edges, C])
        weight1 = sb("weight1", [128, n_product_reads + len(LINEAR_READS) + 1, C])
        ones = sb("ones", [128, 2])
        const1 = sb("const1", [128, 2])
        wr_rows = sb("wr_rows", [C, C * 10])
        wr_out = sb("wr_out", [128, 10])
        b_out = sb("b_out", [128, 3])
        ring_bias = sb("ring_bias", [128, 16])
        stats = sb("stats", [128, PIX // 512, 6])
        mean_var = sb("mean_var", [128, 2])
        norm = sb("norm", [128, 8])
        filt = product[0][0:C, 0:C * M * M].rearrange("p (o m) -> p o m", o=C)
        scratch = product[1]
        w3_in = scratch[0:C, 0:288].rearrange("p (o t) -> p o t", o=C)
        w5_in = scratch[0:C, 288:288 + 800].rearrange("p (o t) -> p o t", o=C)
        w5_sum = product[0][0:C, C * M * M:C * M * M + 800].rearrange("p (o y x) -> p o y x", o=C, y=5)
        shift_w3 = [scratch[0:C, 1088 + 288 * e:1376 + 288 * e].rearrange("p (o y x) -> p o y x", o=C, y=3)
                    for e in range(9)]
        edge_w = [scratch[0:C, 288 + 160 * e:448 + 160 * e].rearrange("p (o t) -> p o t", o=C)
                  for e in range(4)]

        acc0 = ctx.enter_context(nc.psum_tensor("acc0", [128, 2, NCH * CROWS * W], fp32))
        acc1 = ctx.enter_context(nc.psum_tensor("acc1", [128, 2, NCH * CROWS * W], fp32))

        weights_in = sem("weights_in")
        filters_in = sem("filters_in")
        bias_in = sem("bias_in")
        piece_in = [sem(f"piece_in{n}") for n in range(PIECES)]
        raw_in = sem("raw_in")
        x1_in = sem("x1_in")
        resid_in = [sem(f"resid_in{n}") for n in range(len(RESID_PARTS))]
        plane_zero = sem("plane_zero")
        h_rest_zero = sem("h_rest_zero")
        chain = sem("chain")
        var_ready = sem("var_ready")
        std_ready = sem("std_ready")
        plane_ready = sem("plane_ready")
        a_filled = [sem(f"a_filled{i}") for i in range(2)]
        b_filled = sem("b_filled")
        c_filled = [sem(f"c_filled{i}") for i in range(2)]
        h_filled = [sem(f"h_filled{i}") for i in range(2)]
        filled_g = (c_filled[0], a_filled[0], c_filled[1], a_filled[1])
        weight_parts = sem("weight_parts")
        weight0_ready = sem("weight0_ready")
        weight1_ready = sem("weight1_ready")
        const1_sum = sem("const1_sum")
        h_used = sem("h_used")
        conv_done = sem("conv_done")
        x1_ready = sem("x1_ready")
        product_ready = sem("product_ready")
        square_ready = sem("square_ready")
        product_used = sem("product_used")
        out_ready = sem("out_ready")
        stored = sem("stored")

        block = ctx.enter_context(nc.Block())

        EY_EX = [(ey, ex) for ey in (-1, 0, 1) for ex in (-1, 0, 1)]

        def shift_index(ey, ex):
            return 1 + 3 * (1 - ex) + (1 - ey)

        def r_rows(g, shape):
            v = wr_rows[:, :].rearrange("p (o g) -> p o g", g=10)[:, :, g:g + 1]
            return v.to_broadcast(shape)

        def slots(to, kind, bi, on_scalar):
            lo, _ = span[kind]
            for a, s in enumerate(CONV0_SHIFTS.get(kind) or SHIFTS[kind]):
                if (a in ON_SCALAR[kind]) == on_scalar:
                    at = lo + flat(s) - plane_lo
                    yield (to[32 * a:32 * a + 32, 0:size[kind]], plane[32 * bi:32 * bi + 32, at:at + size[kind]])

        def fill(sp, to, kind, bi, done):
            for slot, image in slots(to, kind, bi, False):
                sp.dma_start(slot, image).then_inc(done, 16)

        def fill_on_scalar(to, kind, bi, done):
            for slot, image in slots(to, kind, bi, True):
                nc.scalar.activation(slot, image, ACT.Copy).then_inc(done, 16)

        @block.sync
        def _(sp):
            sp.dma_start(w3_in, w3.rearrange("o c y x -> c o (y x)")).then_inc(weights_in, 16)
            sp.dma_start(w5_in, w5.rearrange("o c y x -> c o (y x)")).then_inc(weights_in, 16)
            for n in range(PIECES):
                sp.dma_start(raw[:, n * PIECE:(n + 1) * PIECE],
                             x[0:GROUP].rearrange("b c h w -> (b c) (h w)")[:, n * PIECE:(n + 1) * PIECE])\
                  .then_inc(piece_in[n], 16)
            with sp.Fori(0, B // GROUP) as g:
                sp.wait_ge(plane_ready, g + 1)
                for bi in range(GROUP):
                    sp.wait_ge(conv_done, g * GROUP + (bi + 1))
                    fill(sp, stack_g[bi], "g", bi, filled_g[bi])
                    sp.wait_ge(h_used, g * GROUP + (bi + 1))
                    if bi == 1:
                        sp.wait_ge(weight0_ready, 2)
                    fill(sp, stack_h[bi % 2], "h", bi, h_filled[bi % 2])
            sp.wait_ge(h_used, AHEAD + B - 1)
            with sp.Fori(0, B // GROUP) as g:
                sp.wait_ge(plane_ready, g + (B // GROUP + 1))
                for bi in range(GROUP):
                    s = bi % 2
                    sp.wait_ge(conv_done, g * GROUP + (CONV_AHEAD + B - AHEAD + bi + 1))
                    fill(sp, stack_a[s], "a", bi, a_filled[s])
                    fill(sp, stack_c[s], "c", bi, c_filled[s])
                    sp.wait_ge(product_ready, g * (GROUP * N_PRODUCTS) + ((AHEAD + bi - 1) * N_PRODUCTS + SQUARED + 1))
                    fill(sp, stack_b, "b", bi, b_filled)

        @block.gpsimd
        def _(pool):
            nc.gpsimd.memset(plane[:, :], 0.0).then_inc(plane_zero, 1)
            nc.gpsimd.memset(ones[:, :], 1.0).then_inc(plane_zero, 1)
            pool.wait_ge(plane_zero, 2)
            for stack in stack_h:
                nc.gpsimd.memset(stack[32 * len(CONV0_SHIFTS["h"]):128, :], 0.0).then_inc(h_rest_zero, 1)
            pool.wait_ge(weights_in, 48)
            for e, (ey, ex) in enumerate(EY_EX):
                nc.gpsimd.tensor_tensor(shift_w3[e].rearrange("p o y x -> p o (y x)"), w3_in,
                                        r_rows(shift_index(ey, ex), (C, C, 9)), ALU.mult)\
                    .then_inc(weight_parts, 1)
            nc.gpsimd.tensor_tensor(w5_sum.rearrange("p o y x -> p o (y x)"), w5_in,
                                    r_rows(0, (C, C, 25)), ALU.mult).then_inc(weight_parts, 1)

            def residual(n, b):
                pool.wait_ge(filled_g[b % GROUP], SLOT_DMA * (b // GROUP + 1))
                first, end = RESID_PARTS[n]
                for q in range(4):
                    pool.dma_start(resid[32 * q:32 * q + 32, first:end, :],
                                  x[first:end].rearrange("b c (q r) w -> q c b (r w)", q=4)[q])\
                       .then_inc(resid_in[n], 16)

            residual(0, 0)
            pool.wait_ge(plane_ready, 1)
            pool.dma_start(raw[:, :], x[GROUP:B].rearrange("b c h w -> (b c) (h w)")).then_inc(raw_in, 16)
            residual(1, 1)
            pool.dma_start(filt, filters.rearrange("o c i j -> c o (i j)")).then_inc(filters_in, 16)
            residual(2, GROUP)
            for g in range(B // GROUP):
                pool.wait_ge(plane_ready, g + 2)
                for bi in range(GROUP):
                    b = GROUP * g + bi
                    pool.wait_ge(x1_ready, AHEAD + b + 1)
                    for q in range(4):
                        pool.dma_start(raw[32 * bi:32 * bi + 32, q * QROWS * W:(q + 1) * QROWS * W],
                                      resid[32 * q:32 * q + 32, b, :]).then_inc(x1_in, 16)
            with pool.Fori(0, B) as b:
                pool.wait_ge(out_ready, b + (AHEAD + 1))
                for q in range(4):
                    pool.dma_start(out[b].rearrange("c (q r) w -> q c (r w)", q=4)[q],
                                  resid[32 * q:32 * q + 32, b, :]).then_inc(stored, 16)
            pool.wait_ge(stored, 16 * 4 * B)

        @block.scalar
        def _(act):
            act.dma_start(wr_rows[:, :], wr.rearrange("o g y x -> (y x) (o g)").to_broadcast((C, C * 10)))\
               .then_inc(weights_in, 16)
            for q in range(4):
                act.dma_start(wr_out[32 * q:32 * q + 32, :], wr.rearrange("o g y x -> o (g y x)"))\
                   .then_inc(bias_in, 16)
                for n, v in enumerate((b3, b5, br)):
                    act.dma_start(b_out[32 * q:32 * q + 32, n:n + 1], v.rearrange("(o n) -> o n", n=1))\
                       .then_inc(bias_in, 16)
            def std(phase):
                act.wait_ge(var_ready, phase + 1)
                nc.scalar.activation(norm[:, 1:2], norm[:, 0:1], ACT.Sqrt).then_inc(std_ready, 1)

            with act.Fori(0, B // GROUP) as g:
                std(g)
                act.wait_ge(plane_ready, g + 1)
                for bi in range(GROUP):
                    act.wait_ge(conv_done, g * GROUP + (bi + 1))
                    fill_on_scalar(stack_g[bi], "g", bi, filled_g[bi])
                    act.wait_ge(h_used, g * GROUP + (bi + 1))
                    if bi == 1:
                        act.wait_ge(weight0_ready, 2)
                    fill_on_scalar(stack_h[bi % 2], "h", bi, h_filled[bi % 2])
            std(2)
            (first, end), u, _, _ = PRODUCTS[SQUARED][0][1]
            low, high = 32 * first, 32 * end
            lo, hi = product_span[SQUARED]
            act.wait_ge(h_used, AHEAD + B - 1)
            for b in range(B):
                s, bi = b % 2, b % GROUP
                act.wait_ge(plane_ready, B // GROUP + b // GROUP + 1)
                act.wait_ge(conv_done, CONV_AHEAD + B - AHEAD + b + 1)
                fill_on_scalar(stack_a[s], "a", bi, a_filled[s])
                fill_on_scalar(stack_c[s], "c", bi, c_filled[s])
                act.wait_ge(product_ready, (AHEAD + b - 1) * N_PRODUCTS + SQUARED + 1)
                fill_on_scalar(stack_b, "b", bi, b_filled)
                if b == GROUP - 1:
                    std(3)
                n = N_PRODUCTS * b + SQUARED
                act.wait_ge(a_filled[s], SLOT_DMA * (B // GROUP + b // 2 + 1))
                act.wait_ge(product_used, n - 1)
                nc.scalar.activation(product[n % 2][low:high, 0:hi - lo + 1],
                                     stack_a[s][low:high, lo - span[u][0]:hi + 1 - span[u][0]], ACT.Square)\
                  .then_inc(square_ready, 1)

        @block.vector
        def _(dve):
            steps = [0]

            def step(ins):
                steps[0] += 1
                ins.then_inc(chain, 1)
                dve.wait_ge(chain, steps[0])

            def statistics(in_pieces=False):
                for n in range(PIX // 512):
                    if in_pieces and 512 * n % PIECE == 0:
                        dve.wait_ge(piece_in[512 * n // PIECE], 16)
                    ins = nc.vector.bn_stats(stats[:, n, :], raw[:, 512 * n:512 * n + 512])
                step(ins)
                step(nc.vector.bn_aggr(mean_var[:, :], stats[:, :, :].rearrange("p n s -> p (n s)")))
                nc.vector.tensor_scalar(norm[:, 0:1], mean_var[:, 1:2], GN_EPS, None, ALU.add)\
                    .then_inc(var_ready, 1)

            def normalise(phase):
                dve.wait_ge(std_ready, phase + 1)
                step(nc.vector.reciprocal(norm[:, 2:3], norm[:, 1:2]))
                step(nc.vector.scalar_tensor_tensor(norm[:, 3:4], norm[:, 2:3], norm[:, 2:3], norm[:, 0:1],
                                                    ALU.mult, ALU.mult))
                step(nc.vector.tensor_scalar(norm[:, 4:5], norm[:, 3:4], -0.5, 1.5, ALU.mult, ALU.add))
                step(nc.vector.tensor_tensor(norm[:, 5:6], norm[:, 2:3], norm[:, 4:5], ALU.mult))
                inner = plane[:, -plane_lo:-plane_lo + H * PITCH].rearrange("p (y x) -> p y x", x=PITCH)[:, :, 0:W]
                nc.vector.tensor_scalar(inner, raw[:, :].rearrange("p (y x) -> p y x", x=W),
                                        mean_var[:, 0:1], norm[:, 5:6], ALU.subtract, ALU.mult)\
                    .then_inc(plane_ready, 1)

            dve.sem_inc(x1_ready, AHEAD)
            dve.sem_inc(product_ready, AHEAD * N_PRODUCTS)
            dve.sem_inc(out_ready, AHEAD - 1)
            nc.vector.memset(weight0[:, :, :], 0.0)
            step(nc.vector.memset(weight_edge[:, :, :], 0.0))
            step(nc.vector.memset(weight1[:, :, :], 0.0))
            statistics(in_pieces=True)
            dve.wait_ge(plane_zero, 1)
            normalise(0)
            dve.wait_ge(weight_parts, len(EY_EX) + 1)
            for e, (ey, ex) in enumerate(EY_EX):
                window = w5_sum[:, :, ey + 1:ey + 4, ex + 1:ex + 4]
                step(nc.vector.tensor_tensor(window, window, shift_w3[e], ALU.add))
            for n, (_, _, mine) in enumerate(taps0):
                for a, (dy, dx) in mine:
                    last = nc.vector.tensor_copy(weight0[32 * a:32 * a + 32, n, :], w5_sum[:, :, dy + 2, dx + 2])
            last.then_inc(weight0_ready, 1)

            def shifted(ey, ex):
                return shift_w3[EY_EX.index((ey, ex))]

            for e in range(4):
                last = nc.vector.memset(edge_w[e], 0.0)
            step(last)
            for e in (-1, 0, 1):
                for side, add in ((0, shifted(-1, e)[:, :, 2, :]), (1, shifted(1, e)[:, :, 0, :]),
                                  (2, shifted(e, -1)[:, :, :, 2]), (3, shifted(e, 1)[:, :, :, 0])):
                    part = edge_w[side][:, :, e + 1:e + 4]
                    last = nc.vector.tensor_tensor(part, part, add, ALU.add)
                step(last)
            n = 0
            for side in range(4):
                for _, mine in (ROW_EDGE if side < 2 else COL_EDGE):
                    for a, t in mine:
                        nc.vector.tensor_scalar(weight_edge[32 * a:32 * a + 32, n, :],
                                                edge_w[side][:, :, t + 2], -1.0, None, ALU.mult)
                    n += 1
            for ey, ex in ((-1, -1), (-1, 1), (1, -1), (1, 1)):
                last = nc.vector.tensor_copy(weight_edge[0:32, n, :], shifted(ey, ex)[:, :, 1 - ey, 1 - ex])
                n += 1
            last.then_inc(weight0_ready, 1)

            dve.wait_ge(bias_in, 16 * 16)
            rb = ring_bias
            step(nc.vector.tensor_scalar(rb[:, 0:9], wr_out[:, 1:10], b_out[:, 0:1], None, ALU.mult))

            def ring(ey, ex):
                i = shift_index(ey, ex) - 1
                return rb[:, i:i + 1]

            step(nc.vector.reduce_sum(rb[:, 9:10], rb[:, 0:9], mybir.AxisListType.X))
            step(nc.vector.scalar_tensor_tensor(rb[:, 9:10], wr_out[:, 0:1], b_out[:, 1:2], rb[:, 9:10],
                                                ALU.mult, ALU.add))
            step(nc.vector.tensor_tensor(rb[:, 9:10], rb[:, 9:10], b_out[:, 2:3], ALU.add))
            for k, three in enumerate((((-1, -1), (-1, 0), (-1, 1)), ((1, -1), (1, 0), (1, 1)),
                                       ((-1, -1), (0, -1), (1, -1)), ((-1, 1), (0, 1), (1, 1)))):
                to = rb[:, 10 + k:11 + k]
                step(nc.vector.tensor_tensor(to, ring(*three[0]), ring(*three[1]), ALU.add))
                step(nc.vector.tensor_tensor(to, to, ring(*three[2]), ALU.add))
            step(nc.vector.memset(bias_map[:, :, :], 0.0))
            step(nc.vector.tensor_scalar(bias_map[:, :, :], bias_map[:, :, :], rb[:, 9:10], None, ALU.add))
            low, high = slice(0, 32), slice(96, 128)
            for p, region, k in ((slice(0, 128), (slice(None), slice(0, 1)), 12),
                                 (slice(0, 128), (slice(None), slice(W - 1, W)), 13),
                                 (low, (slice(0, 1), slice(None)), 10),
                                 (high, (slice(QROWS - 1, QROWS), slice(None)), 11)):
                part = bias_map[p, region[0], region[1]]
                step(nc.vector.tensor_scalar(part, part, rb[p, k:k + 1], None, ALU.subtract))
            for p, row, col, at in ((low, 0, 0, (-1, -1)), (low, 0, W - 1, (-1, 1)),
                                    (high, QROWS - 1, 0, (1, -1)), (high, QROWS - 1, W - 1, (1, 1))):
                part = bias_map[p, row, col:col + 1]
                i = shift_index(*at) - 1
                step(nc.vector.tensor_tensor(part, part, rb[p, i:i + 1], ALU.add))

            flat_bias = bias_map[:, :, :].rearrange("p y x -> p (y x)")
            def finish0(b):
                step(nc.vector.tensor_tensor(resid[:, b, :], resid[:, b, :], flat_bias, ALU.add))
                dve.wait_ge(conv_done, CONV_AHEAD + b + 1)
                nc.vector.tensor_tensor(resid[:, b, :], acc0[:, b % 2, :], resid[:, b, :], ALU.add)\
                    .then_inc(x1_ready, 1)

            def conv1_weights():
                def entry(i, j):
                    return filt[:, :, i * M + j]

                def tap(i):
                    return 1 + 3 * (i[0] + 1) + (i[1] + 1)

                dve.wait_ge(filters_in, 16)
                n = 0
                for rows in taps1:
                    for mine in rows:
                        for a, i, j in mine:
                            to = weight1[32 * a:32 * a + 32, n, :]
                            if i == j:
                                nc.vector.tensor_copy(to, entry(tap(i), tap(i)))
                            else:
                                nc.vector.tensor_tensor(to, entry(tap(i), tap(j)), entry(tap(j), tap(i)), ALU.add)
                        n += 1
                for mine in linear1:
                    for a, i in mine:
                        nc.vector.tensor_tensor(weight1[32 * a:32 * a + 32, n, :],
                                                entry(0, tap(i)), entry(tap(i), 0), ALU.add)
                    n += 1
                nc.vector.tensor_copy(weight1[0:32, n, :], entry(0, 0)).then_inc(weight1_ready, 1)

            def plane_copied(group):
                for s in range(2):
                    fills = min(group, 2) + 2 * max(group - 2, 0)
                    dve.wait_ge(a_filled[s], SLOT_DMA * fills)
                    dve.wait_ge(c_filled[s], SLOT_DMA * fills)
                for i in range(2):
                    dve.wait_ge(h_filled[i], H_DMA * 2 * min(group, 2))
                if group > 2:
                    dve.wait_ge(b_filled, B_DMA * GROUP * (group - 2))

            dve.wait_ge(resid_in[0], 64)
            finish0(0)
            dve.wait_ge(raw_in, 16)
            statistics()
            finish0(1)
            plane_copied(1)
            normalise(1)
            dve.wait_ge(resid_in[1], 64)
            finish0(2)
            finish0(3)
            dve.wait_ge(resid_in[2], 64)
            finish0(4)
            conv1_weights()
            dve.wait_ge(x1_in, 16 * 16)
            statistics()
            finish0(5)
            plane_copied(2)
            normalise(2)
            finish0(6)

            def multiply(b, k):
                (first, end), u, v, d = PRODUCTS[k][0][0]
                low, high = 32 * first, 32 * end
                lo, hi = product_span[k]
                n = N_PRODUCTS * b + k
                at = {"a": stack_a[b % 2], "b": stack_b, "c": stack_c[b % 2]}
                if n >= 2:
                    dve.wait_ge(product_used, n - 1)
                one = at[u][low:high, lo - span[u][0]:hi + 1 - span[u][0]]
                other = at[v][low:high, lo + flat(d) - span[v][0]:hi + 1 + flat(d) - span[v][0]]
                nc.vector.tensor_tensor(product[n % 2][low:high, 0:hi - lo + 1], one, other, ALU.mult)\
                    .then_inc(product_ready, 1)

            def finish1(b):
                dve.wait_ge(conv_done, CONV_AHEAD + B + b + 1)
                nc.vector.scalar_tensor_tensor(resid[:, b, :], acc1[:, b % 2, :], const1[:, 0:1], resid[:, b, :],
                                               ALU.add, ALU.add).then_inc(out_ready, 1)

            for b in range(B):
                s = b % 2
                dve.wait_ge(a_filled[s], SLOT_DMA * (B // GROUP + b // 2 + 1))
                dve.wait_ge(c_filled[s], SLOT_DMA * (B // GROUP + b // 2 + 1))
                multiply(b, 0)
                if b == 0:
                    dve.wait_ge(h_used, AHEAD + B)
                multiply(b, 1)
                if b == 0:
                    finish0(B - 1)
                    dve.wait_ge(const1_sum, 1)
                    nc.vector.tensor_copy(const1[:, :], acc1[:, 1, 0:2]).then_inc(out_ready, 1)
                else:
                    finish1(b - 1)
                if b == GROUP - 2:
                    dve.wait_ge(x1_in, 32 * 16)
                    statistics()
                if b == GROUP - 1:
                    plane_copied(3)
                    normalise(3)
                dve.wait_ge(b_filled, B_DMA * (b + 1))
                for k in range(2, N_PRODUCTS):
                    multiply(b, k)
            finish1(B - 1)

        @block.tensor
        def _(pe):
            def pixels(stack, base, q, h):
                at = base + (QROWS * q + CROWS * h) * PITCH
                return stack[:, at:at + CROWS * PITCH].rearrange("p (y x) -> p y x", x=PITCH)[:, :, 0:W]

            def acc_rows(acc, s, q, h):
                return acc[32 * q:32 * q + 32, s, 512 * h:512 * h + 512]

            def tap_all(acc, s, weights, stack, base, start, stop):
                for h in range(NCH):
                    for q in range(4):
                        last = nc.tensor.matmul(acc_rows(acc, s, q, h), weights, pixels(stack, base, q, h),
                                                start=start, stop=stop, tile_position=(0, 32 * q))
                return last

            g_lo, h_lo = span["g"][0], span["h"][0]

            def row_edges(s, stack):
                n = 0
                for side in range(2):
                    q, h, row = (0, 0, 0) if side == 0 else (3, NCH - 1, CROWS - 1)
                    y = 0 if side == 0 else H - 1
                    for o, _ in ROW_EDGE:
                        at = flat((y, 0)) + flat(o) - g_lo
                        width = W - max(0, o[1]) if side == 1 else W
                        nc.tensor.matmul(acc0[32 * q:32 * q + 32, s, 512 * h + row * W:512 * h + row * W + width],
                                         weight_edge[:, n, :], stack[:, at:at + width],
                                         start=False, stop=False, tile_position=(0, 32 * q))
                        n += 1
                n += 2 * len(COL_EDGE)
                for q, h, row, y in ((0, 0, 0, 0), (3, NCH - 1, CROWS - 1, H - 1)):
                    for col in (0, W - 1):
                        at = flat((y, col)) - g_lo
                        nc.tensor.matmul(acc0[32 * q:32 * q + 32, s, 512 * h + row * W + col:512 * h + row * W + col + 1],
                                         weight_edge[:, n, :], stack[:, at:at + 1],
                                         start=False, stop=False, tile_position=(0, 32 * q))
                        n += 1

            def column_edges(s, stack):
                n = 2 * len(ROW_EDGE)
                for col in (0, W - 1):
                    for o, _ in COL_EDGE:
                        for h in range(NCH):
                            for q in range(4):
                                at = flat((QROWS * q + CROWS * h, col)) + flat(o) - h_lo
                                last = nc.tensor.matmul(acc_rows(acc0, s, q, h)[:, col:col + (CROWS - 1) * W + 1:W],
                                                        weight_edge[:, n, :],
                                                        stack[:, at:at + (CROWS - 1) * PITCH + 1:PITCH],
                                                        start=False, stop=False, tile_position=(0, 32 * q))
                        n += 1
                return last

            pe.sem_inc(h_used, AHEAD)
            pe.sem_inc(conv_done, CONV_AHEAD)
            pe.wait_ge(h_rest_zero, 2)
            pe.wait_ge(weight0_ready, 1)
            with pe.Fori(0, B // GROUP) as g:
                for bi in range(GROUP):
                    s = bi % 2
                    pe.wait_ge(filled_g[bi], g * SLOT_DMA + SLOT_DMA)
                    pe.wait_ge(x1_ready, g * GROUP + (bi + 1))
                    for n, (kind, o, _) in enumerate(taps0):
                        if kind == "h":
                            pe.wait_ge(h_filled[bi % 2], g * (2 * H_DMA) + H_DMA * (bi // 2 + 1))
                        stack = {"g": stack_g[bi], "h": stack_h[bi % 2]}[kind]
                        last = tap_all(acc0, s, weight0[:, n, :], stack, flat(o) - span[kind][0],
                                       n == 0, n == len(taps0) - 1)
                        if kind == "h":
                            pe.wait_ge(weight0_ready, 2)
                            column_edges(s, stack_h[bi % 2]).then_inc(h_used, 1)
                            row_edges(s, stack_g[bi])
                    last.then_inc(conv_done, 1)

            pe.wait_ge(weight1_ready, 1)
            pe.wait_ge(plane_zero, 2)
            for q in range(4):
                last = nc.tensor.matmul(acc1[32 * q:32 * q + 32, 1, 0:2], weight1[:, N_READS, :], ones[:, :],
                                        start=True, stop=True, tile_position=(0, 32 * q))
            last.then_inc(const1_sum, 1)

            with pe.Fori(0, B // 2) as i:
                for s in range(2):
                    n = 0
                    pe.wait_ge(out_ready, i * 2 + (s + 1))
                    linear = 0
                    for k, (_, reads) in enumerate(PRODUCTS):
                        pe.wait_ge(product_ready, i * (2 * N_PRODUCTS) + ((AHEAD + s) * N_PRODUCTS + k + 1))
                        if k == SQUARED:
                            pe.wait_ge(square_ready, i * 2 + (s + 1))
                        for o in reads:
                            last = tap_all(acc1, s, weight1[:, n, :], product[(N_PRODUCTS * s + k) % 2],
                                           flat(o) - product_span[k][0], n == 0, False)
                            n += 1
                        last.then_inc(product_used, 1)
                        for o in LINEAR_READS[linear:linear + LINEAR_AFTER[k]]:
                            last = tap_all(acc1, s, weight1[:, n_product_reads + linear, :], stack_a[s],
                                           flat(o) - span["a"][0], False, linear == len(LINEAR_READS) - 1)
                            linear += 1
                    last.then_inc(conv_done, 1)


def kernel(**inputs):
    import numpy as np
    import concourse.bacc as bacc
    from concourse.bass_utils import run_bass_kernel_spmd

    nc = bacc.Bacc("TRN2", target_bir_lowering=False, num_devices=1)
    names = ("x", "L0_conv_w3", "L0_conv_b3", "L0_conv_w5", "L0_conv_b5", "L0_conv_wr", "L0_conv_br",
             "L1_conv_filters")
    arrays, args = {}, []
    for name in names:
        a = np.ascontiguousarray(inputs[name])
        arrays[f"in_{name}"] = a
        args.append(nc.dram_tensor(f"in_{name}", a.shape, mybir.dt.from_np(a.dtype), kind="ExternalInput").ap())
    out = nc.dram_tensor("out", (B, C, H, W), mybir.dt.float32, kind="ExternalOutput").ap()
    conv_kernel(nc, *args, out)
    r = run_bass_kernel_spmd(nc, [arrays], core_ids=[0])
    return r.results[0]["out"]
```

```python
from contextlib import ExitStack

import concourse.bass as bass
from concourse import mybir

B, C, H, W = 8, 32, 64, 64
SLOTS = 4
GROUP = 4
PITCH = W + 2
PIX = H * W
LAST = (H - 1) * PITCH + W - 1
QROWS = H // 4
CROWS = 8
NCH = QROWS // CROWS
GN_EPS = 1e-5


def flat(p):
    return p[0] * PITCH + p[1]


CONV0_SHIFTS = {"g": ((0, 0), (0, 1), (1, 1), (1, 2)), "h": ((-2, 0), (0, 0), (2, 0))}
CONV0_READS = (("g", (-2, -1)), ("g", (-2, 1)), ("h", (0, -2)), ("g", (-1, -2)), ("g", (0, 1)), ("g", (1, -2)),
               ("g", (1, 0)))


def conv0_taps():
    seen, out = set(), []
    for kind, o in CONV0_READS:
        mine = []
        for a, s in enumerate(CONV0_SHIFTS[kind]):
            tap = (o[0] + s[0], o[1] + s[1])
            if max(abs(tap[0]), abs(tap[1])) <= 2 and tap not in seen:
                seen.add(tap)
                mine.append((a, tap))
        out.append((kind, o, mine))
    assert len(seen) == 25
    return out


ROW_EDGE = (((0, -2), ((0, -2), (1, -1))), ((0, 0), ((0, 0), (1, 1))), ((0, 2), ((0, 2),)))
COL_EDGE = (((0, 0), ((0, -2), (1, 0), (2, 2))), ((1, 0), ((0, -1), (1, 1))))

SHIFTS = {
    "a": ((0, 0), (1, 0), (0, 0), (2, 0)),
    "c": ((2, 0), (1, 0), (1, 0), (1, 0)),
    "b": ((2, 0), (0, 0)),
}
SQUARES = ((0, 2), "b", "b", (0, 0))
PRODUCTS = (
    ((SQUARES, ((2, 4), "a", "c", (1, 1))), ((-1, -1), (-1, 0))),
    ((SQUARES, ((2, 4), "a", "c", (1, -2))), ((-1, 1),)),
    ((((0, 4), "a", "c", (-1, 1)),), ((-1, 0), (-1, -1), (0, -1), (0, 0))),
    ((((0, 4), "a", "c", (0, 0)),), ((-1, 1), (-1, -1), (-1, 0))),
    ((((0, 4), "a", "c", (-1, -2)),), ((-1, 1), (0, 1))),
)
SQUARED = tuple(k for k, (parts, _) in enumerate(PRODUCTS) if parts[0] == SQUARES)
LINEAR_READS = ((-1, 1), (-1, 0), (-1, -1))
LINEAR_AFTER = (1, 1, 0, 0, 1)

ON_SCALAR = {"g": (2,), "h": (2,), "a": (3,), "c": (3,), "b": (1,)}
ON_VECTOR = {"g": (3,)}


def inside(p):
    return abs(p[0]) <= 1 and abs(p[1]) <= 1


def conv1_taps():
    seen, out = set(), []
    for parts, reads in PRODUCTS:
        rows = []
        for o in reads:
            mine = []
            for (first, end), u, v, d in parts:
                for a in range(first, end):
                    i = (o[0] + SHIFTS[u][a][0], o[1] + SHIFTS[u][a][1])
                    j = (o[0] + SHIFTS[v][a][0] + d[0], o[1] + SHIFTS[v][a][1] + d[1])
                    pair = tuple(sorted((i, j)))
                    if inside(i) and inside(j) and pair not in seen:
                        seen.add(pair)
                        mine.append((a, i, j))
            rows.append(mine)
        out.append(rows)
    assert len(seen) == 45
    lin, linear = set(), []
    for o in LINEAR_READS:
        mine = []
        for a in range(SLOTS):
            i = (o[0] + SHIFTS["a"][a][0], o[1] + SHIFTS["a"][a][1])
            if inside(i) and i not in lin:
                lin.add(i)
                mine.append((a, i))
        linear.append(mine)
    assert len(lin) == 9
    return out, linear


def ranges():
    need = {"g": [(-2, LAST + 2)], "h": [(0, LAST + flat((1, 0)))],
            "a": [(min(map(flat, LINEAR_READS)), LAST + max(map(flat, LINEAR_READS)))], "b": [], "c": []}
    for kind, o in CONV0_READS:
        need[kind].append((flat(o), LAST + flat(o)))
    products = []
    for parts, reads in PRODUCTS:
        lo, hi = min(map(flat, reads)), LAST + max(map(flat, reads))
        products.append((lo, hi))
        for _, u, v, d in parts:
            need[u].append((lo, hi))
            need[v].append((lo + flat(d), hi + flat(d)))
    span = {k: (min(lo for lo, _ in r), max(hi for _, hi in r)) for k, r in need.items()}
    shifts = dict(SHIFTS, **CONV0_SHIFTS)
    plane = (min(span[k][0] + flat(s) for k in span for s in shifts[k]),
             max(span[k][1] + flat(s) for k in span for s in shifts[k]))
    return span, products, plane


def conv_kernel(nc, x, w3, b3, w5, b5, wr, br, filters, out):
    fp32 = mybir.dt.float32
    ALU = mybir.AluOpType
    ACT = mybir.ActivationFunctionType

    span, product_span, (plane_lo, plane_hi) = ranges()
    plane_len = plane_hi - plane_lo + 1
    size = {k: hi - lo + 1 for k, (lo, hi) in span.items()}
    taps0 = conv0_taps()
    taps1, linear1 = conv1_taps()
    n_product_reads = sum(len(reads) for _, reads in PRODUCTS)
    M = filters.shape[2]
    N_READS = n_product_reads + len(LINEAR_READS)
    SLOT_DMA = 16 * SLOTS
    B_DMA = 16 * len(SHIFTS["b"])
    H_DMA = 16 * len(CONV0_SHIFTS["h"])
    AHEAD = 2
    CONV_AHEAD = 4
    RESID_PARTS = ((0, 2), (2, GROUP), (GROUP, B))
    PIECES = 4
    PIECE = PIX // PIECES
    N_PRODUCTS = len(PRODUCTS)
    N_SQUARES = len(SQUARED)

    ctx = ExitStack()
    with ctx:
        def sb(name, shape):
            return ctx.enter_context(nc.sbuf_tensor(name, shape, fp32))

        def sem(name):
            return ctx.enter_context(nc.semaphore(name))

        raw = sb("raw", [128, PIX])
        plane = sb("plane", [128, plane_len])
        stack_a = [sb(f"stack_a{i}", [128, max(size["a"], size["g"]) + PITCH - W]) for i in range(2)]
        stack_b = sb("stack_b", [128, max(size["b"], size["h"]) + PITCH - W])
        stack_c = [sb(f"stack_c{i}", [128, max(size["c"], size["g"]) + PITCH - W]) for i in range(2)]
        product = [sb(f"product{i}", [128, max(hi - lo + 1 for lo, hi in product_span) + PITCH - W]) for i in range(2)]
        stack_g = (stack_c[0], stack_a[0], stack_c[1], stack_a[1])
        stack_h = (stack_b, product[1])
        h_rest = [stack[32 * len(CONV0_SHIFTS["h"]):128, :] for stack in stack_h]
        resid = sb("resid", [128, B, QROWS * W])
        bias_map = sb("bias_map", [128, QROWS, W])
        weight0 = sb("weight0", [128, len(taps0), C])
        n_edges = 2 * len(ROW_EDGE) + 2 * len(COL_EDGE) + 4
        weight_edge = sb("weight_edge", [128, n_edges, C])
        weight1 = sb("weight1", [128, n_product_reads + len(LINEAR_READS) + 1, C])
        ones = sb("ones", [128, 2])
        warm = sb("warm", [128, 2])
        const1 = sb("const1", [128, 2])
        wr_rows = sb("wr_rows", [C, C * 10])
        wr_out = sb("wr_out", [128, 10])
        b_out = sb("b_out", [128, 3])
        ring_bias = sb("ring_bias", [128, 16])
        stats = sb("stats", [128, PIX // 512, 6])
        mean_var = sb("mean_var", [128, 2])
        norm = sb("norm", [128, 8])
        filt = product[0][0:C, 0:C * M * M].rearrange("p (o m) -> p o m", o=C)
        scratch = product[1]
        w3_in = scratch[0:C, 0:288].rearrange("p (o t) -> p o t", o=C)
        w5_in = scratch[0:C, 288:288 + 800].rearrange("p (o t) -> p o t", o=C)
        w5_sum = product[0][0:C, C * M * M:C * M * M + 800].rearrange("p (o y x) -> p o y x", o=C, y=5)
        shift_w3 = [scratch[0:C, 1088 + 288 * e:1376 + 288 * e].rearrange("p (o y x) -> p o y x", o=C, y=3)
                    for e in range(9)]
        edge_w = [scratch[0:C, 288 + 160 * e:448 + 160 * e].rearrange("p (o t) -> p o t", o=C)
                  for e in range(4)]

        acc0 = ctx.enter_context(nc.psum_tensor("acc0", [128, 2, NCH * CROWS * W], fp32))
        acc1 = ctx.enter_context(nc.psum_tensor("acc1", [128, 2, NCH * CROWS * W], fp32))

        columns = acc1[:, :, 512:512 + 2 * QROWS].rearrange("p s (e r) -> p s e r", e=2)

        weights_in = sem("weights_in")
        filters_in = sem("filters_in")
        bias_in = sem("bias_in")
        piece_in = [sem(f"piece_in{n}") for n in range(PIECES)]
        raw_in = sem("raw_in")
        x1_in = sem("x1_in")
        resid_in = [sem(f"resid_in{n}") for n in range(len(RESID_PARTS))]
        plane_zero = sem("plane_zero")
        h_rest_zero = sem("h_rest_zero")
        chain = sem("chain")
        warmed = sem("warmed")
        var_ready = sem("var_ready")
        std_ready = sem("std_ready")
        plane_ready = sem("plane_ready")
        a_filled = [sem(f"a_filled{i}") for i in range(2)]
        b_filled = sem("b_filled")
        c_filled = [sem(f"c_filled{i}") for i in range(2)]
        h_filled = [sem(f"h_filled{i}") for i in range(2)]
        filled_g = (c_filled[0], a_filled[0], c_filled[1], a_filled[1])
        weight_parts = sem("weight_parts")
        weight0_ready = sem("weight0_ready")
        weight1_ready = sem("weight1_ready")
        const1_sum = sem("const1_sum")
        h_used = sem("h_used")
        conv_done = sem("conv_done")
        half_done = sem("half_done")
        x1_ready = sem("x1_ready")
        product_ready = sem("product_ready")
        square_ready = sem("square_ready")
        product_used = sem("product_used")
        out_ready = sem("out_ready")
        half_ready = sem("half_ready")
        stored = sem("stored")
        last_stored = sem("last_stored")

        block = ctx.enter_context(nc.Block())

        EY_EX = [(ey, ex) for ey in (-1, 0, 1) for ex in (-1, 0, 1)]
        ON_POOL = 7

        def shift_index(ey, ex):
            return 1 + 3 * (1 - ex) + (1 - ey)

        def r_rows(g, shape):
            v = wr_rows[:, :].rearrange("p (o g) -> p o g", g=10)[:, :, g:g + 1]
            return v.to_broadcast(shape)

        def slots(to, kind, bi, mine):
            lo, _ = span[kind]
            shifts = CONV0_SHIFTS.get(kind) or SHIFTS[kind]
            for a in mine:
                at = lo + flat(shifts[a]) - plane_lo
                yield (to[32 * a:32 * a + 32, 0:size[kind]], plane[32 * bi:32 * bi + 32, at:at + size[kind]])

        def store_last(eng, quarters):
            for h in range(NCH):
                eng.wait_ge(half_ready, h + 1)
                for q in quarters:
                    eng.dma_start(out[B - 1].rearrange("c (q h r) w -> q h c (r w)", q=4, h=NCH)[q, h],
                                  resid[32 * q:32 * q + 32, B - 1, 512 * h:512 * h + 512]).then_inc(last_stored, 16)

        def fill(sp, to, kind, bi, done):
            n = len(CONV0_SHIFTS.get(kind) or SHIFTS[kind])
            mine = [a for a in range(n) if a not in ON_SCALAR[kind] + ON_VECTOR.get(kind, ())]
            for slot, image in slots(to, kind, bi, mine):
                sp.dma_start(slot, image).then_inc(done, 16)

        def fill_on_scalar(to, kind, bi, done):
            for slot, image in slots(to, kind, bi, ON_SCALAR[kind]):
                nc.scalar.activation(slot, image, ACT.Copy).then_inc(done, 16)

        @block.sync
        def _(sp):
            sp.dma_start(w3_in, w3.rearrange("o c y x -> c o (y x)")).then_inc(weights_in, 16)
            sp.dma_start(w5_in, w5.rearrange("o c y x -> c o (y x)")).then_inc(weights_in, 16)
            for n in range(PIECES):
                sp.dma_start(raw[:, n * PIECE:(n + 1) * PIECE],
                             x[0:GROUP].rearrange("b c h w -> (b c) (h w)")[:, n * PIECE:(n + 1) * PIECE])\
                  .then_inc(piece_in[n], 16)
            for q in range(4):
                sp.dma_start(wr_out[32 * q:32 * q + 32, :], wr.rearrange("o g y x -> o (g y x)"))\
                   .then_inc(bias_in, 16)
                for n, v in enumerate((b3, b5, br)):
                    sp.dma_start(b_out[32 * q:32 * q + 32, n:n + 1], v.rearrange("(o n) -> o n", n=1))\
                       .then_inc(bias_in, 16)
            with sp.Fori(0, B // GROUP) as g:
                sp.wait_ge(plane_ready, g + 1)
                for bi in range(GROUP):
                    sp.wait_ge(conv_done, g * GROUP + (bi + 1))
                    fill(sp, stack_g[bi], "g", bi, filled_g[bi])
                    sp.wait_ge(h_used, g * GROUP + (bi + 1))
                    if bi == 1:
                        sp.wait_ge(weight0_ready, 2)
                    fill(sp, stack_h[bi % 2], "h", bi, h_filled[bi % 2])
            sp.wait_ge(h_used, AHEAD + B - 1)
            with sp.Fori(0, B // GROUP) as g:
                sp.wait_ge(plane_ready, g + (B // GROUP + 1))
                for bi in range(GROUP):
                    s = bi % 2
                    if bi == 0:
                        sp.wait_ge(conv_done, g * (GROUP + 1) + (CONV_AHEAD + B - AHEAD))
                    else:
                        sp.wait_ge(conv_done, g * GROUP + (CONV_AHEAD + B - AHEAD + bi + 1))
                    fill(sp, stack_a[s], "a", bi, a_filled[s])
                    fill(sp, stack_c[s], "c", bi, c_filled[s])
                    sp.wait_ge(square_ready, g * (GROUP * N_SQUARES) + (AHEAD + bi) * N_SQUARES)
                    fill(sp, stack_b, "b", bi, b_filled)
            store_last(sp, (0, 1))

        @block.gpsimd
        def _(pool):
            nc.gpsimd.memset(ones[:, :], 1.0).then_inc(plane_zero, 1)
            nc.gpsimd.memset(plane[:, 0:-plane_lo], 0.0).then_inc(plane_zero, 1)
            nc.gpsimd.memset(plane[:, H * PITCH - plane_lo:plane_len], 0.0).then_inc(plane_zero, 1)
            nc.gpsimd.memset(plane[:, -plane_lo:H * PITCH - plane_lo].rearrange("p (y x) -> p y x", x=PITCH)[:, :, W:PITCH],
                             0.0).then_inc(plane_zero, 1)
            pool.wait_ge(weights_in, 48)
            for e, (ey, ex) in enumerate(EY_EX):
                nc.gpsimd.tensor_tensor(shift_w3[e].rearrange("p o y x -> p o (y x)"), w3_in,
                                        r_rows(shift_index(ey, ex), (C, C, 9)), ALU.mult)\
                    .then_inc(weight_parts, 1)
            nc.gpsimd.tensor_tensor(w5_sum.rearrange("p o y x -> p o (y x)"), w5_in,
                                    r_rows(0, (C, C, 25)), ALU.mult).then_inc(weight_parts, 1)
            for e, (ey, ex) in enumerate(EY_EX[:ON_POOL]):
                pool.wait_ge(weight_parts, len(EY_EX) + 1 + e)
                window = w5_sum[:, :, ey + 1:ey + 4, ex + 1:ex + 4]
                nc.gpsimd.tensor_tensor(window, window, shift_w3[e], ALU.add).then_inc(weight_parts, 1)
            for rest in h_rest:
                nc.gpsimd.memset(rest, 0.0).then_inc(h_rest_zero, 1)

            def residual(n, b):
                pool.wait_ge(filled_g[b % GROUP], SLOT_DMA * (b // GROUP + 1))
                first, end = RESID_PARTS[n]
                for q in range(4):
                    pool.dma_start(resid[32 * q:32 * q + 32, first:end, :],
                                  x[first:end].rearrange("b c (q r) w -> q c b (r w)", q=4)[q])\
                       .then_inc(resid_in[n], 16)

            residual(0, 0)
            pool.wait_ge(plane_ready, 1)
            pool.dma_start(raw[:, :], x[GROUP:B].rearrange("b c h w -> (b c) (h w)")).then_inc(raw_in, 16)
            residual(1, 1)
            pool.dma_start(filt, filters.rearrange("o c i j -> c o (i j)")).then_inc(filters_in, 16)
            residual(2, GROUP)
            for g in range(B // GROUP):
                pool.wait_ge(plane_ready, g + 2)
                for bi in range(GROUP):
                    b = GROUP * g + bi
                    pool.wait_ge(x1_ready, AHEAD + b + 1)
                    for q in range(4):
                        pool.dma_start(raw[32 * bi:32 * bi + 32, q * QROWS * W:(q + 1) * QROWS * W],
                                      resid[32 * q:32 * q + 32, b, :]).then_inc(x1_in, 16)
            with pool.Fori(0, B - 1) as b:
                pool.wait_ge(out_ready, b + (AHEAD + 1))
                for q in range(4):
                    pool.dma_start(out[b].rearrange("c (q r) w -> q c (r w)", q=4)[q],
                                  resid[32 * q:32 * q + 32, b, :]).then_inc(stored, 16)
            pool.wait_ge(stored, 16 * 4 * (B - 1))
            pool.wait_ge(last_stored, 16 * 4 * NCH)

        @block.scalar
        def _(act):
            act.dma_start(wr_rows[:, :], wr.rearrange("o g y x -> (y x) (o g)").to_broadcast((C, C * 10)))\
               .then_inc(weights_in, 16)
            act.wait_ge(plane_zero, 1)
            nc.scalar.activation(warm[:, :], ones[:, :], ACT.Sqrt).then_inc(warmed, 1)

            def std(phase):
                act.wait_ge(var_ready, phase + 1)
                nc.scalar.activation(norm[:, 1:2], norm[:, 0:1], ACT.Sqrt).then_inc(std_ready, 1)

            with act.Fori(0, B // GROUP) as g:
                std(g)
                act.wait_ge(plane_ready, g + 1)
                for bi in range(GROUP):
                    act.wait_ge(conv_done, g * GROUP + (bi + 1))
                    fill_on_scalar(stack_g[bi], "g", bi, filled_g[bi])
                    act.wait_ge(h_used, g * GROUP + (bi + 1))
                    if bi == 1:
                        act.wait_ge(weight0_ready, 2)
                    fill_on_scalar(stack_h[bi % 2], "h", bi, h_filled[bi % 2])
            std(2)
            (first, end), _, _, _ = SQUARES
            low, high = 32 * first, 32 * end
            for b in range(B):
                s, bi = b % 2, b % GROUP
                act.wait_ge(plane_ready, B // GROUP + b // GROUP + 1)
                act.wait_ge(conv_done, CONV_AHEAD + B - AHEAD + (b + 1 if b else 0))
                fill_on_scalar(stack_a[s], "a", bi, a_filled[s])
                fill_on_scalar(stack_c[s], "c", bi, c_filled[s])
                act.wait_ge(square_ready, (AHEAD + b) * N_SQUARES)
                if b == 0:
                    act.wait_ge(h_used, AHEAD + B - 1)
                fill_on_scalar(stack_b, "b", bi, b_filled)
                if b == GROUP - 1:
                    std(3)
                act.wait_ge(b_filled, B_DMA * (b + 1))
                for k in SQUARED:
                    n = N_PRODUCTS * b + k
                    lo, hi = product_span[k]
                    if n >= 2:
                        act.wait_ge(product_used, n - 1)
                    elif n == 1:
                        act.wait_ge(h_used, AHEAD + B)
                    else:
                        act.wait_ge(weight1_ready, 1)
                    nc.scalar.activation(product[n % 2][low:high, 0:hi - lo + 1],
                                         stack_b[low:high, lo - span["b"][0]:hi + 1 - span["b"][0]], ACT.Square)\
                      .then_inc(square_ready, 1)
            store_last(act, (2, 3))

        @block.vector
        def _(dve):
            steps = [0]

            def step(ins):
                steps[0] += 1
                ins.then_inc(chain, 1)
                dve.wait_ge(chain, steps[0])

            def statistics(in_pieces=False, first=0, end=PIX // 512):
                for n in range(first, end):
                    if in_pieces and 512 * n % PIECE == 0:
                        dve.wait_ge(piece_in[512 * n // PIECE], 16)
                    ins = nc.vector.bn_stats(stats[:, n, :], raw[:, 512 * n:512 * n + 512])
                if end < PIX // 512:
                    return
                step(ins)
                step(nc.vector.bn_aggr(mean_var[:, :], stats[:, :, :].rearrange("p n s -> p (n s)")))
                nc.vector.tensor_scalar(norm[:, 0:1], mean_var[:, 1:2], GN_EPS, None, ALU.add)\
                    .then_inc(var_ready, 1)

            def normalise(phase):
                dve.wait_ge(std_ready, phase + 1)
                step(nc.vector.reciprocal(norm[:, 2:3], norm[:, 1:2]))
                step(nc.vector.scalar_tensor_tensor(norm[:, 3:4], norm[:, 2:3], norm[:, 2:3], norm[:, 0:1],
                                                    ALU.mult, ALU.mult))
                step(nc.vector.tensor_scalar(norm[:, 4:5], norm[:, 3:4], -0.5, 1.5, ALU.mult, ALU.add))
                step(nc.vector.tensor_tensor(norm[:, 5:6], norm[:, 2:3], norm[:, 4:5], ALU.mult))
                inner = plane[:, -plane_lo:-plane_lo + H * PITCH].rearrange("p (y x) -> p y x", x=PITCH)[:, :, 0:W]
                nc.vector.tensor_scalar(inner, raw[:, :].rearrange("p (y x) -> p y x", x=W),
                                        mean_var[:, 0:1], norm[:, 5:6], ALU.subtract, ALU.mult)\
                    .then_inc(plane_ready, 1)

            def copy_g(b):
                dve.wait_ge(plane_ready, b // GROUP + 1)
                if b >= GROUP:
                    dve.wait_ge(conv_done, b + 1)
                for slot, image in slots(stack_g[b % GROUP], "g", b % GROUP, ON_VECTOR["g"]):
                    nc.vector.tensor_copy(slot, image).then_inc(filled_g[b % GROUP], 16)

            dve.sem_inc(x1_ready, AHEAD)
            dve.sem_inc(product_ready, AHEAD * N_PRODUCTS)
            dve.sem_inc(square_ready, AHEAD * N_SQUARES)
            dve.sem_inc(out_ready, AHEAD - 1)
            nc.vector.memset(weight0[:, :, :], 0.0)
            step(nc.vector.memset(weight_edge[:, :, :], 0.0))
            step(nc.vector.memset(weight1[:, :, :], 0.0))
            statistics(in_pieces=True)
            dve.wait_ge(plane_zero, 4)
            normalise(0)
            copy_g(0)
            dve.wait_ge(weight_parts, len(EY_EX) + 1 + ON_POOL)
            for e, (ey, ex) in enumerate(EY_EX[ON_POOL:]):
                window = w5_sum[:, :, ey + 1:ey + 4, ex + 1:ex + 4]
                step(nc.vector.tensor_tensor(window, window, shift_w3[ON_POOL + e], ALU.add))
            for n, (_, _, mine) in enumerate(taps0):
                for a, (dy, dx) in mine:
                    last = nc.vector.tensor_copy(weight0[32 * a:32 * a + 32, n, :], w5_sum[:, :, dy + 2, dx + 2])
            last.then_inc(weight0_ready, 1)
            copy_g(1)

            def shifted(ey, ex):
                return shift_w3[EY_EX.index((ey, ex))]

            for e in range(4):
                last = nc.vector.memset(edge_w[e], 0.0)
            step(last)
            for e in (-1, 0, 1):
                for side, add in ((0, shifted(-1, e)[:, :, 2, :]), (1, shifted(1, e)[:, :, 0, :]),
                                  (2, shifted(e, -1)[:, :, :, 2]), (3, shifted(e, 1)[:, :, :, 0])):
                    part = edge_w[side][:, :, e + 1:e + 4]
                    last = nc.vector.tensor_tensor(part, part, add, ALU.add)
                step(last)
            n = 0
            for side in range(4):
                for _, mine in (ROW_EDGE if side < 2 else COL_EDGE):
                    for a, t in mine:
                        nc.vector.tensor_scalar(weight_edge[32 * a:32 * a + 32, n, :],
                                                edge_w[side][:, :, t + 2], -1.0, None, ALU.mult)
                    n += 1
            for ey, ex in ((-1, -1), (-1, 1), (1, -1), (1, 1)):
                last = nc.vector.tensor_copy(weight_edge[0:32, n, :], shifted(ey, ex)[:, :, 1 - ey, 1 - ex])
                n += 1
            last.then_inc(weight0_ready, 1)

            copy_g(2)
            copy_g(3)

            dve.wait_ge(bias_in, 16 * 16)
            rb = ring_bias
            step(nc.vector.tensor_scalar(rb[:, 0:9], wr_out[:, 1:10], b_out[:, 0:1], None, ALU.mult))

            def ring(ey, ex):
                i = shift_index(ey, ex) - 1
                return rb[:, i:i + 1]

            step(nc.vector.reduce_sum(rb[:, 9:10], rb[:, 0:9], mybir.AxisListType.X))
            step(nc.vector.scalar_tensor_tensor(rb[:, 9:10], wr_out[:, 0:1], b_out[:, 1:2], rb[:, 9:10],
                                                ALU.mult, ALU.add))
            step(nc.vector.tensor_tensor(rb[:, 9:10], rb[:, 9:10], b_out[:, 2:3], ALU.add))
            for k, three in enumerate((((-1, -1), (-1, 0), (-1, 1)), ((1, -1), (1, 0), (1, 1)),
                                       ((-1, -1), (0, -1), (1, -1)), ((-1, 1), (0, 1), (1, 1)))):
                to = rb[:, 10 + k:11 + k]
                step(nc.vector.tensor_tensor(to, ring(*three[0]), ring(*three[1]), ALU.add))
                step(nc.vector.tensor_tensor(to, to, ring(*three[2]), ALU.add))
            step(nc.vector.memset(bias_map[:, :, :], 0.0))
            step(nc.vector.tensor_scalar(bias_map[:, :, :], bias_map[:, :, :], rb[:, 9:10], None, ALU.add))
            low, high = slice(0, 32), slice(96, 128)
            for p, region, k in ((slice(0, 128), (slice(None), slice(0, 1)), 12),
                                 (slice(0, 128), (slice(None), slice(W - 1, W)), 13),
                                 (low, (slice(0, 1), slice(None)), 10),
                                 (high, (slice(QROWS - 1, QROWS), slice(None)), 11)):
                part = bias_map[p, region[0], region[1]]
                step(nc.vector.tensor_scalar(part, part, rb[p, k:k + 1], None, ALU.subtract))
            for p, row, col, at in ((low, 0, 0, (-1, -1)), (low, 0, W - 1, (-1, 1)),
                                    (high, QROWS - 1, 0, (1, -1)), (high, QROWS - 1, W - 1, (1, 1))):
                part = bias_map[p, row, col:col + 1]
                i = shift_index(*at) - 1
                step(nc.vector.tensor_tensor(part, part, rb[p, i:i + 1], ALU.add))

            flat_bias = bias_map[:, :, :].rearrange("p y x -> p (y x)")
            def finish0(b):
                step(nc.vector.tensor_tensor(resid[:, b, :], resid[:, b, :], flat_bias, ALU.add))
                dve.wait_ge(h_used, AHEAD + b + 1)
                sides = resid[:, b, :].rearrange("p (r w) -> p w r", w=W)[:, 0:W:W - 1, :]
                step(nc.vector.tensor_tensor(sides, columns[:, b % 2, :, :], sides, ALU.add))
                dve.wait_ge(conv_done, CONV_AHEAD + b + 1)
                nc.vector.tensor_tensor(resid[:, b, :], acc0[:, b % 2, :], resid[:, b, :], ALU.add)\
                    .then_inc(x1_ready, 1)

            def conv1_weights():
                def entry(i, j):
                    return filt[:, :, i * M + j]

                def tap(i):
                    return 1 + 3 * (i[0] + 1) + (i[1] + 1)

                dve.wait_ge(filters_in, 16)
                n = 0
                for rows in taps1:
                    for mine in rows:
                        for a, i, j in mine:
                            to = weight1[32 * a:32 * a + 32, n, :]
                            if i == j:
                                nc.vector.tensor_copy(to, entry(tap(i), tap(i)))
                            else:
                                nc.vector.tensor_tensor(to, entry(tap(i), tap(j)), entry(tap(j), tap(i)), ALU.add)
                        n += 1
                for mine in linear1:
                    for a, i in mine:
                        nc.vector.tensor_tensor(weight1[32 * a:32 * a + 32, n, :],
                                                entry(0, tap(i)), entry(tap(i), 0), ALU.add)
                    n += 1
                nc.vector.tensor_copy(weight1[0:32, n, :], entry(0, 0)).then_inc(weight1_ready, 1)

            def plane_copied(group):
                for s in range(2):
                    fills = min(group, 2) + 2 * max(group - 2, 0)
                    dve.wait_ge(a_filled[s], SLOT_DMA * fills)
                    dve.wait_ge(c_filled[s], SLOT_DMA * fills)
                for i in range(2):
                    dve.wait_ge(h_filled[i], H_DMA * 2 * min(group, 2))
                if group > 2:
                    dve.wait_ge(b_filled, B_DMA * GROUP * (group - 2))

            dve.wait_ge(resid_in[0], 64)
            finish0(0)
            dve.wait_ge(raw_in, 16)
            statistics()
            finish0(1)
            plane_copied(1)
            normalise(1)
            copy_g(4)
            dve.wait_ge(resid_in[1], 64)
            copy_g(5)
            finish0(2)
            copy_g(6)
            finish0(3)
            copy_g(7)
            dve.wait_ge(resid_in[2], 64)
            finish0(4)
            conv1_weights()
            dve.wait_ge(x1_in, 16 * 16)
            statistics()
            finish0(5)
            plane_copied(2)
            normalise(2)
            finish0(6)

            def multiply(b, k):
                (first, end), u, v, d = PRODUCTS[k][0][-1]
                low, high = 32 * first, 32 * end
                lo, hi = product_span[k]
                n = N_PRODUCTS * b + k
                at = {"a": stack_a[b % 2], "b": stack_b, "c": stack_c[b % 2]}
                if n >= 2:
                    dve.wait_ge(product_used, n - 1)
                one = at[u][low:high, lo - span[u][0]:hi + 1 - span[u][0]]
                other = at[v][low:high, lo + flat(d) - span[v][0]:hi + 1 + flat(d) - span[v][0]]
                nc.vector.tensor_tensor(product[n % 2][low:high, 0:hi - lo + 1], one, other, ALU.mult)\
                    .then_inc(product_ready, 1)

            def finish1(b):
                dve.wait_ge(conv_done, CONV_AHEAD + B + b + 1)
                nc.vector.scalar_tensor_tensor(resid[:, b, :], acc1[:, b % 2, :], const1[:, 0:1], resid[:, b, :],
                                               ALU.add, ALU.add).then_inc(out_ready, 1)

            for b in range(B):
                s = b % 2
                dve.wait_ge(a_filled[s], SLOT_DMA * (B // GROUP + b // 2 + 1))
                dve.wait_ge(c_filled[s], SLOT_DMA * (B // GROUP + b // 2 + 1))
                multiply(b, 0)
                if b == 0:
                    dve.wait_ge(h_used, AHEAD + B)
                multiply(b, 1)
                if b == 0:
                    finish0(B - 1)
                    dve.wait_ge(const1_sum, 1)
                    nc.vector.tensor_copy(const1[:, :], acc1[:, 1, 0:2]).then_inc(out_ready, 1)
                if b == 2:
                    statistics(first=7)
                multiply(b, 2)
                multiply(b, 3)
                if b > 0:
                    finish1(b - 1)
                if b == 1:
                    dve.wait_ge(x1_in, 32 * 16)
                    statistics(end=5)
                if b == GROUP - 2:
                    plane_copied(3)
                    normalise(3)
                multiply(b, 4)
                if b == 1:
                    statistics(first=5, end=7)
            for h in range(NCH):
                if h == 0:
                    dve.wait_ge(half_done, B)
                else:
                    dve.wait_ge(conv_done, CONV_AHEAD + 2 * B)
                half = slice(512 * h, 512 * h + 512)
                nc.vector.scalar_tensor_tensor(resid[:, B - 1, half], acc1[:, (B - 1) % 2, half], const1[:, 0:1],
                                               resid[:, B - 1, half], ALU.add, ALU.add).then_inc(half_ready, 1)

        @block.tensor
        def _(pe):
            def pixels(stack, base, q, h):
                at = base + (QROWS * q + CROWS * h) * PITCH
                return stack[:, at:at + CROWS * PITCH].rearrange("p (y x) -> p y x", x=PITCH)[:, :, 0:W]

            def acc_rows(acc, s, q, h):
                return acc[32 * q:32 * q + 32, s, 512 * h:512 * h + 512]

            def tap_all(acc, s, weights, stack, base, start, stop, halves=range(NCH)):
                for h in halves:
                    for q in range(4):
                        last = nc.tensor.matmul(acc_rows(acc, s, q, h), weights, pixels(stack, base, q, h),
                                                start=start, stop=stop, tile_position=(0, 32 * q))
                return last

            g_lo, h_lo = span["g"][0], span["h"][0]

            def row_edges(s, stack):
                n = 0
                for side in range(2):
                    q, h, row = (0, 0, 0) if side == 0 else (3, NCH - 1, CROWS - 1)
                    y = 0 if side == 0 else H - 1
                    for o, _ in ROW_EDGE:
                        at = flat((y, 0)) + flat(o) - g_lo
                        width = W - max(0, o[1]) if side == 1 else W
                        nc.tensor.matmul(acc0[32 * q:32 * q + 32, s, 512 * h + row * W:512 * h + row * W + width],
                                         weight_edge[:, n, :], stack[:, at:at + width],
                                         start=False, stop=False, tile_position=(0, 32 * q))
                        n += 1
                n += 2 * len(COL_EDGE)
                for q, h, row, y in ((0, 0, 0, 0), (3, NCH - 1, CROWS - 1, H - 1)):
                    for col in (0, W - 1):
                        at = flat((y, col)) - g_lo
                        nc.tensor.matmul(acc0[32 * q:32 * q + 32, s, 512 * h + row * W + col:512 * h + row * W + col + 1],
                                         weight_edge[:, n, :], stack[:, at:at + 1],
                                         start=False, stop=False, tile_position=(0, 32 * q))
                        n += 1

            def column_edges(s, stack):
                n = 2 * len(ROW_EDGE)
                for side, col in enumerate((0, W - 1)):
                    for k, (o, _) in enumerate(COL_EDGE):
                        for q in range(4):
                            at = flat((QROWS * q, col)) + flat(o) - h_lo
                            last = nc.tensor.matmul(columns[32 * q:32 * q + 32, s, side, :], weight_edge[:, n, :],
                                                    stack[:, at:at + (QROWS - 1) * PITCH + 1:PITCH],
                                                    start=k == 0, stop=k == len(COL_EDGE) - 1,
                                                    tile_position=(0, 32 * q))
                        n += 1
                return last

            pe.sem_inc(h_used, AHEAD)
            pe.sem_inc(conv_done, CONV_AHEAD)
            pe.wait_ge(weight0_ready, 1)
            with pe.Fori(0, B // GROUP) as g:
                for bi in range(GROUP):
                    s = bi % 2
                    pe.wait_ge(filled_g[bi], g * SLOT_DMA + SLOT_DMA)
                    pe.wait_ge(x1_ready, g * GROUP + (bi + 1))
                    for n, (kind, o, _) in enumerate(taps0):
                        if kind == "h":
                            pe.wait_ge(h_rest_zero, 2)
                            pe.wait_ge(h_filled[bi % 2], g * (2 * H_DMA) + H_DMA * (bi // 2 + 1))
                        stack = {"g": stack_g[bi], "h": stack_h[bi % 2]}[kind]
                        last = tap_all(acc0, s, weight0[:, n, :], stack, flat(o) - span[kind][0],
                                       n == 0, n == len(taps0) - 1)
                        if kind == "h":
                            pe.wait_ge(weight0_ready, 2)
                            column_edges(s, stack_h[bi % 2]).then_inc(h_used, 1)
                            row_edges(s, stack_g[bi])
                    last.then_inc(conv_done, 1)

            pe.wait_ge(weight1_ready, 1)
            pe.wait_ge(plane_zero, 1)
            for q in range(4):
                last = nc.tensor.matmul(acc1[32 * q:32 * q + 32, 1, 0:2], weight1[:, N_READS, :], ones[:, :],
                                        start=True, stop=True, tile_position=(0, 32 * q))
            last.then_inc(const1_sum, 1)

            with pe.Fori(0, B // 2) as i:
                for s in range(2):
                    n = 0
                    pe.wait_ge(out_ready, i * 2 + (s + 1))
                    linear = 0
                    for k, (_, reads) in enumerate(PRODUCTS):
                        pe.wait_ge(product_ready, i * (2 * N_PRODUCTS) + ((AHEAD + s) * N_PRODUCTS + k + 1))
                        if k in SQUARED:
                            pe.wait_ge(square_ready, i * (2 * N_SQUARES) + ((AHEAD + s) * N_SQUARES
                                                                            + SQUARED.index(k) + 1))
                        for o in reads:
                            last = tap_all(acc1, s, weight1[:, n, :], product[(N_PRODUCTS * s + k) % 2],
                                           flat(o) - product_span[k][0], n == 0, False)
                            n += 1
                        last.then_inc(product_used, 1)
                        mine = range(linear, linear + LINEAR_AFTER[k])
                        linear += LINEAR_AFTER[k]
                        for halves in ((0,), (1,)) if k == N_PRODUCTS - 1 else ((0, 1),):
                            for m in mine:
                                last = tap_all(acc1, s, weight1[:, n_product_reads + m, :], stack_a[s],
                                               flat(LINEAR_READS[m]) - span["a"][0], False,
                                               m == len(LINEAR_READS) - 1, halves)
                            if halves == (0,):
                                last.then_inc(half_done, 1)
                    last.then_inc(conv_done, 1)


def kernel(**inputs):
    import numpy as np
    import concourse.bacc as bacc
    from concourse.bass_utils import run_bass_kernel_spmd

    nc = bacc.Bacc("TRN2", target_bir_lowering=False, num_devices=1)
    names = ("x", "L0_conv_w3", "L0_conv_b3", "L0_conv_w5", "L0_conv_b5", "L0_conv_wr", "L0_conv_br",
             "L1_conv_filters")
    arrays, args = {}, []
    for name in names:
        a = np.ascontiguousarray(inputs[name])
        arrays[f"in_{name}"] = a
        args.append(nc.dram_tensor(f"in_{name}", a.shape, mybir.dt.from_np(a.dtype), kind="ExternalInput").ap())
    out = nc.dram_tensor("out", (B, C, H, W), mybir.dt.float32, kind="ExternalOutput").ap()
    conv_kernel(nc, *args, out)
    r = run_bass_kernel_spmd(nc, [arrays], core_ids=[0])
    return r.results[0]["out"]
```
